# Optimizing a Trainium2 kernel written in Bass

```python
import numpy as np
import jax
import jax.numpy as jnp

def _softmax(x, axis=-1):
    return jax.nn.softmax(x, axis=axis)
def _gelu(x):
    return jax.nn.gelu(x, approximate=True)
def _silu(x):
    return jax.nn.silu(x)
def _sigmoid(x):
    return jax.nn.sigmoid(x)
def _layernorm(x, axis=-1, eps=1e-5):
    m = jnp.mean(x, axis=axis, keepdims=True)
    v = jnp.var(x, axis=axis, keepdims=True)
    return (x - m) / jnp.sqrt(v + eps)
def _scatter_add(tgt, idx, src, axis=0):
    return tgt.at[idx].add(src)
def _segment_sum(src, seg, n):
    return jax.ops.segment_sum(src, seg, n)

kernel_name = 'mk_conv_preact_d1_conv_nchw256_464486'

def setup_inputs(seed: int = 0):
    np.random.seed(seed)
    _w = jnp.asarray
    def _rec_inputs():
        import jax
        import jax.numpy as jnp
        _gk = jax.random.key(seed)
        x = -0.0003929 + 0.9999 * jax.random.normal(jax.random.fold_in(_gk, 1), (4, 256, 128, 128), jnp.float32)
        return x
    x = _rec_inputs()
    def _L0_conv_setup():
        import jax, jax.numpy as jnp
        import numpy as np
        DIM = 256
        HEADS = 8
        DH = DIM // HEADS
        BLOCK = 8
        HALO = 3
        WIN = BLOCK + 2 * HALO

        def _halo_attention(x, w_q, w_kv, fc_w, fc_b, rel_h, rel_w):
            B, C, H, Wd = x.shape
            nbh, nbw = (H // BLOCK, Wd // BLOCK)
            nb = nbh * nbw
            q = jnp.einsum('oc,bchw->bohw', w_q, x)
            kv = jnp.einsum('oc,bchw->bohw', w_kv, x)
            qb = q.reshape(B, C, nbh, BLOCK, nbw, BLOCK).transpose(0, 2, 4, 3, 5, 1).reshape(B, nb, BLOCK * BLOCK, C)
            kvp = jnp.pad(kv, ((0, 0), (0, 0), (HALO, HALO), (HALO, HALO)))
            ih = (jnp.arange(nbh) * BLOCK)[:, None] + jnp.arange(WIN)[None, :]
            iw = (jnp.arange(nbw) * BLOCK)[:, None] + jnp.arange(WIN)[None, :]
            win = kvp[:, :, ih[:, None, :, None], iw[None, :, None, :]]
            win = win.transpose(0, 2, 3, 4, 5, 1).reshape(B, nb, WIN * WIN, 2 * C)
            k, v = (win[..., :C], win[..., C:])
            qh = qb.reshape(B, nb, BLOCK * BLOCK, HEADS, DH).transpose(0, 1, 3, 2, 4)
            kh = k.reshape(B, nb, WIN * WIN, HEADS, DH).transpose(0, 1, 3, 2, 4)
            vh = v.reshape(B, nb, WIN * WIN, HEADS, DH).transpose(0, 1, 3, 2, 4)
            score = jnp.einsum('bnhqd,bnhkd->bnhqk', qh * DH ** (-0.5), kh)
            q2 = qh.reshape(B, nb, HEADS, BLOCK, BLOCK, DH)
            idx = jnp.arange(WIN)[None, :] - jnp.arange(BLOCK)[:, None] + (WIN - 1)
            bias_w = jnp.einsum('bnhxyd,yjd->bnhxyj', q2, rel_w[idx])
            bias_h = jnp.einsum('bnhxyd,xid->bnhxyi', q2, rel_h[idx])
            bias = bias_w[..., None, :] + bias_h[..., :, None]
            bias = bias.reshape(B, nb, HEADS, BLOCK * BLOCK, WIN * WIN)
            att = jax.nn.softmax(score + bias, axis=-1)
            ctx = jnp.einsum('bnhqk,bnhkd->bnhqd', att, vh)
            ctx = ctx.transpose(0, 1, 3, 2, 4).reshape(B, nb, BLOCK * BLOCK, C)
            out = jnp.einsum('bnqc,oc->bnqo', ctx, fc_w) + fc_b
            out = out.reshape(B, nbh, nbw, BLOCK, BLOCK, C).transpose(0, 5, 1, 3, 2, 4).reshape(B, C, H, Wd)
            return out
        key = jax.random.key(seed)
        ks = jax.random.split(key, 7)
        x = jax.random.normal(ks[0], (4, DIM, 128, 128), jnp.float32)
        w_q = jax.random.normal(ks[1], (DIM, DIM), jnp.float32) * DIM ** (-0.5)
        w_kv = jax.random.normal(ks[2], (2 * DIM, DIM), jnp.float32) * DIM ** (-0.5)
        fc_w = jax.random.normal(ks[3], (DIM, DIM), jnp.float32) * DIM ** (-0.5)
        fc_b = jax.random.normal(ks[4], (DIM,), jnp.float32) * 0.01
        rel_h = jax.random.normal(ks[5], (2 * WIN - 1, DH), jnp.float32) * DH ** (-0.5)
        rel_w = jax.random.normal(ks[6], (2 * WIN - 1, DH), jnp.float32) * DH ** (-0.5)
        return dict(x=x, w_q=w_q, w_kv=w_kv, fc_w=fc_w, fc_b=fc_b, rel_h=rel_h, rel_w=rel_w)
    _L0_conv_all = _L0_conv_setup()
    _L0_conv_in = {k: v for k, v in _L0_conv_all.items() if k in ('w_q', 'w_kv', 'fc_w', 'fc_b', 'rel_h', 'rel_w', )}
    del _L0_conv_all

    return {
        "x": x,
        "L0_conv_w_q": _L0_conv_in["w_q"],
        "L0_conv_w_kv": _L0_conv_in["w_kv"],
        "L0_conv_fc_w": _L0_conv_in["fc_w"],
        "L0_conv_fc_b": _L0_conv_in["fc_b"],
        "L0_conv_rel_h": _L0_conv_in["rel_h"],
        "L0_conv_rel_w": _L0_conv_in["rel_w"],
    }

def reference(x, L0_conv_w_q, L0_conv_w_kv, L0_conv_fc_w, L0_conv_fc_b, L0_conv_rel_h, L0_conv_rel_w):
    import jax
    import jax.numpy as jnp
    def _L0_conv_ref(x, w_q, w_kv, fc_w, fc_b, rel_h, rel_w):
        import jax, jax.numpy as jnp
        import numpy as np
        DIM = 256
        HEADS = 8
        DH = DIM // HEADS
        BLOCK = 8
        HALO = 3
        WIN = BLOCK + 2 * HALO

        def _halo_attention(x, w_q, w_kv, fc_w, fc_b, rel_h, rel_w):
            B, C, H, Wd = x.shape
            nbh, nbw = (H // BLOCK, Wd // BLOCK)
            nb = nbh * nbw
            q = jnp.einsum('oc,bchw->bohw', w_q, x)
            kv = jnp.einsum('oc,bchw->bohw', w_kv, x)
            qb = q.reshape(B, C, nbh, BLOCK, nbw, BLOCK).transpose(0, 2, 4, 3, 5, 1).reshape(B, nb, BLOCK * BLOCK, C)
            kvp = jnp.pad(kv, ((0, 0), (0, 0), (HALO, HALO), (HALO, HALO)))
            ih = (jnp.arange(nbh) * BLOCK)[:, None] + jnp.arange(WIN)[None, :]
            iw = (jnp.arange(nbw) * BLOCK)[:, None] + jnp.arange(WIN)[None, :]
            win = kvp[:, :, ih[:, None, :, None], iw[None, :, None, :]]
            win = win.transpose(0, 2, 3, 4, 5, 1).reshape(B, nb, WIN * WIN, 2 * C)
            k, v = (win[..., :C], win[..., C:])
            qh = qb.reshape(B, nb, BLOCK * BLOCK, HEADS, DH).transpose(0, 1, 3, 2, 4)
            kh = k.reshape(B, nb, WIN * WIN, HEADS, DH).transpose(0, 1, 3, 2, 4)
            vh = v.reshape(B, nb, WIN * WIN, HEADS, DH).transpose(0, 1, 3, 2, 4)
            score = jnp.einsum('bnhqd,bnhkd->bnhqk', qh * DH ** (-0.5), kh)
            q2 = qh.reshape(B, nb, HEADS, BLOCK, BLOCK, DH)
            idx = jnp.arange(WIN)[None, :] - jnp.arange(BLOCK)[:, None] + (WIN - 1)
            bias_w = jnp.einsum('bnhxyd,yjd->bnhxyj', q2, rel_w[idx])
            bias_h = jnp.einsum('bnhxyd,xid->bnhxyi', q2, rel_h[idx])
            bias = bias_w[..., None, :] + bias_h[..., :, None]
            bias = bias.reshape(B, nb, HEADS, BLOCK * BLOCK, WIN * WIN)
            att = jax.nn.softmax(score + bias, axis=-1)
            ctx = jnp.einsum('bnhqk,bnhkd->bnhqd', att, vh)
            ctx = ctx.transpose(0, 1, 3, 2, 4).reshape(B, nb, BLOCK * BLOCK, C)
            out = jnp.einsum('bnqc,oc->bnqo', ctx, fc_w) + fc_b
            out = out.reshape(B, nbh, nbw, BLOCK, BLOCK, C).transpose(0, 5, 1, 3, 2, 4).reshape(B, C, H, Wd)
            return out
        return _halo_attention(x, w_q, w_kv, fc_w, fc_b, rel_h, rel_w)

    def _gn(v, G=32, eps=1e-5):
        B_, C_, H_, W_ = v.shape
        g = v.reshape(B_, G, C_ // G, H_, W_)
        m = jnp.mean(g, axis=(2, 3, 4), keepdims=True)
        s = jnp.var(g, axis=(2, 3, 4), keepdims=True)
        return ((g - m) / jnp.sqrt(s + eps)).reshape(v.shape)

    def _ln_c(v, eps=1e-6):
        m = jnp.mean(v, axis=1, keepdims=True)
        s = jnp.var(v, axis=1, keepdims=True)
        return (v - m) / jnp.sqrt(s + eps)

    def _ln_t(v, eps=1e-5):
        m = jnp.mean(v, axis=-1, keepdims=True)
        s = jnp.var(v, axis=-1, keepdims=True)
        return (v - m) / jnp.sqrt(s + eps)

    def _to_tokens(v):
        B_, C_, H_, W_ = v.shape
        return v.reshape(B_, C_, H_ * W_).transpose(0, 2, 1)
    def _from_tokens(t, like):
        B_, C_, H_, W_ = like.shape
        return t.transpose(0, 2, 1).reshape(B_, C_, H_, W_)

    x = x + _L0_conv_ref(_gn(x), L0_conv_w_q, L0_conv_w_kv, L0_conv_fc_w, L0_conv_fc_b, L0_conv_rel_h, L0_conv_rel_w)
    return x


_drawn_inputs = setup_inputs


def setup_inputs(seed=0):
    import zlib

    import numpy as np

    out = dict(_drawn_inputs(seed))
    spreads = {}
    factors = {'L0_conv_fc_b': 5.961}
    for name, (base, spread) in spreads.items():
        noise = np.random.default_rng([zlib.crc32(name.encode()), seed]).standard_normal(out[name].shape)
        drawn = base * np.exp(spread * noise) if base else spread * noise
        out[name] = jnp.asarray(drawn.astype(out[name].dtype))
    for name, factor in factors.items():
        out[name] = (out[name] * factor).astype(out[name].dtype)
    return out
```

```python
from contextlib import ExitStack

import concourse.bass as bass
from concourse import mybir

F32 = mybir.dt.float32
F16 = mybir.dt.float16
ALU = mybir.AluOpType
ACT = mybir.ActivationFunctionType
AX = mybir.AxisListType

P = 128
C, H, W = 256, 128, 128
HEADS, DH = 8, 32
BLK, HALO = 8, 3
WIN = BLK + 2 * HALO
NKEY = WIN * WIN
NQ = BLK * BLK
GROUPS, GN_EPS = 32, 1e-5
CG = C // GROUPS
KC = C // P
ROWS = H // BLK
TURNS = W // BLK // 2
WP = W + BLK
CHUNK = BLK * WIN
CHUNKS = WP // BLK
PADK = 2 * CHUNK
PAIRS = HEADS // 2
PIX = BLK * W
NREL = 3 * BLK
WS = 64.0
SCALE = float(DH) ** -0.5
FILLS_Q, FILLS_K, FILLS_V, FILLS_B = 4, 4, 9, 4
FILLS = FILLS_Q + FILLS_K + FILLS_V + FILLS_B
NWORD = 6


def halo_attention_program(nc, x, wqT, wkT, wvT, fcT, fcb, rel, onehot, ident_in, gmean_in, out):
    B = x.shape[0]
    IMG_FILLS = FILLS_K + ROWS * FILLS

    with ExitStack() as ctx:
        def sb(name, shape, dt):
            return ctx.enter_context(nc.sbuf_tensor(name, shape, dt))

        def psum(name):
            return ctx.enter_context(nc.psum_tensor(name, [P, 512], F32))

        def sem(name):
            return ctx.enter_context(nc.semaphore(name))

        ident = sb("ident", [P, P], F32)
        gmean = sb("gmean", [P, P], F32)
        w32 = sb("w32", [P, NREL * P], F32)
        w_hi = {n: sb(f"w{n}_hi", [P, KC, C], F16) for n in "qkvo"}
        w_lo = {n: sb(f"w{n}_lo", [P, KC, C], F16) for n in "qkvo"}
        rel_hi = sb("rel_hi", [P, NREL, P], F16)
        rel_lo = sb("rel_lo", [P, NREL, P], F16)
        fcb_sb = sb("fcb_sb", [P, KC], F32)
        x_load = sb("x_load", [P, KC, BLK, W], F32)
        x_norm = sb("x_norm", [P, KC, BLK, W], F32)
        st_load = sb("st_load", [P, KC * PIX], F32)
        stats = sb("stats", [P, ROWS, TURNS, NWORD], F32)
        gn = sb("gn", [P, 8, KC], F32)
        agg = sb("agg", [P, KC, 2], F32)
        mean_sb = sb("mean_sb", [P, KC], F32)
        rstd_sb = sb("rstd_sb", [P, KC], F32)
        xn_hi = sb("xn_hi", [P, KC, WP, WIN], F16)
        xn_lo = sb("xn_lo", [P, KC, WP, WIN], F16)
        k_hi = sb("k_hi", [P, PAIRS, WP, WIN], F16)
        k_lo = sb("k_lo", [P, PAIRS, WP, WIN], F16)
        q_hi = sb("q_hi", [P, 2, 2, TURNS * NQ], F16)
        q_lo = sb("q_lo", [P, 2, 2, TURNS * NQ], F16)
        b_hi = sb("b_hi", [P, 2, 2, TURNS * NQ], F16)
        b_lo = sb("b_lo", [P, 2, 2, TURNS * NQ], F16)
        qd_hi = sb("qd_hi", [P, PAIRS, 2, TURNS, 2, NQ], F16)
        qd_lo = sb("qd_lo", [P, PAIRS, 2, TURNS, 2, NQ], F16)
        v_hi = sb("v_hi", [CHUNK, CHUNKS, C], F16)
        v_lo = sb("v_lo", [CHUNK, CHUNKS, C], F16)
        negmax = sb("negmax", [P, 4, 2], F32)
        rowsum = sb("rowsum", [P, 4, 2], F32)
        rinv = sb("rinv", [P, 4, 2], F32)
        prob = sb("prob", [P, 2, 2, PADK], F32)
        pt_hi = sb("pt_hi", [CHUNK, 2, 512], F16)
        pt_lo = sb("pt_lo", [CHUNK, 2, 512], F16)
        ctxn = sb("ctxn", [P, 2, PAIRS, DH], F32)
        ct_hi = sb("ct_hi", [P, 2, 2, NQ], F16)
        ct_lo = sb("ct_lo", [P, 2, 2, NQ], F16)
        res = sb("res", [P, KC, BLK, W], F32)

        ps_s = [psum(f"ps_scores{i}") for i in range(2)]
        ps_t = [psum(f"ps_probT{i}") for i in range(2)]
        ps_c = psum("ps_context")
        ps_f = psum("ps_output")
        ps_p = [psum(f"ps_project{i}") for i in range(2)]

        weights_in = sem("weights_in")
        consts_in = sem("consts_in")
        split_hi = sem("split_hi")
        split_lo = sem("split_lo")
        zeroed = sem("zeroed")
        onehot_in = sem("onehot_in")
        st_in = sem("st_in")
        st_read = sem("st_read")
        gn_step = sem("gn_step")
        gn_mean = sem("gn_mean")
        gn_ready = sem("gn_ready")
        x_in = sem("x_in")
        x_read = sem("x_read")
        pool_step = sem("pool_step")
        xn_ready = sem("xn_ready")
        res_in = sem("res_in")
        res_ready = sem("res_ready")
        out_stored = sem("out_stored")
        pool_went_on = sem("pool_went_on")
        dve_went_on = sem("dve_went_on")
        fill_done = sem("fill_done")
        fill_hi = sem("fill_hi")
        fill_lo = sem("fill_lo")
        k_down = sem("k_down")
        qd_ready = sem("qd_ready")
        bd_ready = sem("bd_ready")
        scores_ready = sem("scores_ready")
        max_ready = sem("max_ready")
        exp_done = sem("exp_done")
        rinv_done = sem("rinv_done")
        probT_ready = sem("probT_ready")
        pt_hi_done = sem("pt_hi_done")
        pt_lo_done = sem("pt_lo_done")
        context_done = sem("context_done")
        norm_done = sem("norm_done")
        ctxT_ready = sem("ctxT_ready")
        ct_hi_done = sem("ct_hi_done")
        ct_lo_done = sem("ct_lo_done")
        fc_done = sem("fc_done")
        out_added = sem("out_added")

        CREDITS = [(exp_done, 2), (probT_ready, 2), (rinv_done, 4), (pt_lo_done, 2), (context_done, 2),
                   (norm_done, 1), (ctxT_ready, 1), (fc_done, 1), (out_added, 1), (fill_done, 1),
                   (fill_lo, 2), (st_read, 1), (x_read, 1), (out_stored, 16)]
        NZERO = 8
        scratch = sb("scratch", [P, len(CREDITS)], F32)
        mhalf = sb("mhalf", [P, KC], F32)

        block = ctx.enter_context(nc.Block())

        def fills_before(img, s):
            return img * IMG_FILLS + FILLS_K + (s - 1) * FILLS

        @block.sync
        def _(sp):
            sp.dma_start(ident[:, :], ident_in).then_inc(consts_in, 16)
            sp.dma_start(gmean[:, :], gmean_in).then_inc(consts_in, 16)
            sp.dma_start(fcb_sb[:, :], fcb).then_inc(consts_in, 16)
            for n, w in enumerate((wqT, wkT, wvT, fcT, rel)):
                if n:
                    sp.wait_ge(split_lo, n)
                sp.dma_start(w32[:, 0:w.shape[1]], w).then_inc(weights_in, 16)
            sp.wait_ge(zeroed, NZERO)
            for p in range(PAIRS):
                r0 = 64 if p % 2 == 0 else 0
                sp.dma_start(k_hi[r0:r0 + 64, p, :, :], onehot[r0:r0 + 64, :, :]).then_inc(onehot_in, 16)

            x_pix = x.rearrange("b (k p) h w -> p b k (h w)", p=P)
            out_pix = out.rearrange("b (k p) h w -> p b k (h w)", p=P)

            def load_stats(img, r, piece):
                sp.wait_ge(st_read, piece * TURNS + 1)
                sp.dma_start(st_load[:, :].rearrange("p (k n) -> p k n", k=KC),
                             x_pix[:, bass.ds(img, 1), :, bass.ds(r * PIX, PIX)]
                             .rearrange("p a k n -> p (a k) n")).then_inc(st_in, 16)

            def load_strip(img, s, first_row, to_row, rows):
                sp.wait_ge(x_read, img * (ROWS + 1) + s + 1)
                for k in range(KC):
                    sp.dma_start(x_load[:, k, to_row:to_row + rows, :].rearrange("p r w -> p (r w)"),
                                 x_pix[:, bass.ds(img, 1), k, bass.ds(first_row * W, rows * W)]
                                 .rearrange("p a n -> p (a n)")).then_inc(x_in, 16)

            def load_residual(img, s):
                sp.wait_ge(out_stored, ((img * ROWS + s - 1) * KC + 1) * 16)
                for k in range(KC):
                    sp.dma_start(res[:, k, :, :].rearrange("p r w -> p (r w)"),
                                 x_pix[:, bass.ds(img, 1), k, bass.ds((s - 1) * PIX, PIX)]
                                 .rearrange("p a n -> p (a n)")).then_inc(res_in, 16)

            def store_row(img, s):
                sp.wait_ge(out_added, (img * ROWS + s) * TURNS + 1)
                for k in range(KC):
                    sp.dma_start(out_pix[:, bass.ds(img, 1), k, bass.ds((s - 1) * PIX, PIX)]
                                 .rearrange("p a n -> p (a n)"),
                                 res[:, k, :, :].rearrange("p r w -> p (r w)")).then_inc(out_stored, 16)

            with sp.Fori(0, ROWS) as r:
                load_stats(0, r, r)
            with sp.Fori(0, B) as img:
                load_strip(img, 0, 0, BLK - HALO, HALO)
                load_strip(img, 1, HALO, 0, BLK)
                with sp.Fori(1, ROWS - 1) as s:
                    load_residual(img, s)
                    load_stats((img + 1) % B, s - 1, (img + 1) * ROWS + s - 1)
                    load_strip(img, s + 1, s * BLK + HALO, 0, BLK)
                    store_row(img, s)
                for s in (ROWS - 1, ROWS):
                    load_residual(img, s)
                    load_stats((img + 1) % B, s - 1, (img + 1) * ROWS + s - 1)
                    if s < ROWS:
                        load_strip(img, s + 1, s * BLK + HALO, 0, BLK - HALO)
                    store_row(img, s)
            sp.wait_ge(out_stored, (B * ROWS * KC + 1) * 16)

        @block.gpsimd
        def _(pool):
            g = nc.gpsimd
            g.memset(k_hi[:, :, :, :], 0.0).then_inc(zeroed, 1)
            g.memset(k_lo[:, :, :, :], 0.0).then_inc(zeroed, 1)
            g.memset(xn_hi[:, :, :, :], 0.0).then_inc(zeroed, 1)
            g.memset(xn_lo[:, :, :, :], 0.0).then_inc(zeroed, 1)
            g.memset(qd_hi[:, :, :, :, :, :], 0.0).then_inc(zeroed, 1)
            g.memset(qd_lo[:, :, :, :, :, :], 0.0).then_inc(zeroed, 1)
            g.memset(prob[:, :, :, :], 0.0).then_inc(zeroed, 1)
            g.memset(mhalf[:, :], -0.5).then_inc(zeroed, 1)
            for at, (s, n) in enumerate(CREDITS):
                g.memset(scratch[:, at:at + 1], 0.0).then_inc(s, n)
            pool.wait_ge(zeroed, NZERO)
            pool.wait_ge(consts_in, 48)

            inner = slice(HALO, HALO + W)
            keep = WIN - BLK

            def prepare_strip(img, s, kind):
                n = img * (ROWS + 1) + s
                if kind == "first":
                    pool.wait_ge(fill_done, img * IMG_FILLS + 1)
                    pool.sem_inc(pool_went_on, 1)
                    g.memset(xn_hi[:, :, :, keep:WIN - HALO], 0.0)
                    g.memset(xn_lo[:, :, :, keep:WIN - HALO], 0.0).then_inc(pool_step, 2)
                    pool.wait_ge(gn_step, 6 * img + 6)
                    pool.sem_inc(pool_went_on, 1)
                    g.tensor_tensor(rstd_sb[:, :], gn[:, 3, :], mhalf[:, :], ALU.pow).then_inc(gn_ready, 1)
                    pool.wait_ge(gn_ready, img + 1)
                    pool.sem_inc(pool_went_on, 1)
                    at, rows, frm = WIN - HALO, HALO, BLK - HALO
                else:
                    read = img * IMG_FILLS + FILLS_K if kind == "second" else \
                        fills_before(img, s - 1) + FILLS_Q + FILLS_K + FILLS_V
                    pool.wait_ge(fill_done, read + 1)
                    pool.sem_inc(pool_went_on, 1)
                    g.tensor_scalar(xn_hi[:, :, :, 0:keep], xn_hi[:, :, :, BLK:WIN], 1.0, None, ALU.mult)
                    copied = g.tensor_scalar(xn_lo[:, :, :, 0:keep], xn_lo[:, :, :, BLK:WIN], 1.0, None,
                                             ALU.mult)
                    at, rows, frm = keep, BLK, 0
                    if kind == "last":
                        copied.then_inc(pool_step, 1)
                        pool.wait_ge(pool_step, 3 * n + 1)
                        pool.sem_inc(pool_went_on, 1)
                        rows = BLK - HALO
                        g.memset(xn_hi[:, :, :, WIN - HALO:WIN], 0.0)
                        g.memset(xn_lo[:, :, :, WIN - HALO:WIN], 0.0).then_inc(pool_step, 1)
                    else:
                        copied.then_inc(pool_step, 2)
                pool.wait_ge(x_in, (n + 1) * KC * 16)
                pool.sem_inc(pool_went_on, 1)
                for k in range(KC):
                    done = g.tensor_scalar(x_norm[:, k, frm:frm + rows, :], x_load[:, k, frm:frm + rows, :],
                                           mean_sb[:, k:k + 1], rstd_sb[:, k:k + 1],
                                           ALU.subtract, ALU.mult)
                done.then_inc(x_read, 1)
                pool.wait_ge(x_read, n + 2)
                pool.wait_ge(pool_step, 3 * n + 2)
                pool.sem_inc(pool_went_on, 1)
                columns = x_norm[:, :, frm:frm + rows, :].rearrange("p k r w -> p k w r")
                for k in range(KC):
                    done = g.tensor_scalar(xn_hi[:, k, inner, at:at + rows], columns[:, k, :, :], 1.0, None,
                                           ALU.mult)
                done.then_inc(pool_step, 1)
                pool.wait_ge(pool_step, 3 * n + 3)
                pool.sem_inc(pool_went_on, 1)
                for k in range(KC):
                    done = g.tensor_tensor(xn_lo[:, k, inner, at:at + rows], columns[:, k, :, :],
                                           xn_hi[:, k, inner, at:at + rows], ALU.subtract)
                done.then_inc(xn_ready, 1)

            def row(img, s):
                rr = img * ROWS + s - 1
                pool.wait_ge(xn_ready, img * (ROWS + 1) + s + 1)
                for par in range(2):
                    pool.wait_ge(fill_lo, fills_before(img, s) + 2 * par + 2 + 2)
                    pool.sem_inc(pool_went_on, 1)
                    for hq in range(4):
                        r = slice(32 * hq, 32 * hq + 32)
                        for to, frm in ((qd_hi, q_hi), (qd_lo, q_lo)):
                            done = g.tensor_scalar(to[r, hq // 2::2, par, :, hq % 2, :],
                                                   frm[r, :, par, :].rearrange("p g (t q) -> p g t q", q=NQ),
                                                   1.0, None, ALU.mult)
                    done.then_inc(qd_ready, 1)
                pool.wait_ge(qd_ready, 2 * rr + 2)
                pool.wait_ge(res_in, (rr + 1) * KC * 16)
                pool.sem_inc(pool_went_on, 1)
                for k in range(KC):
                    done = g.tensor_scalar(res[:, k, :, :], res[:, k, :, :], fcb_sb[:, k:k + 1], None, ALU.add)
                done.then_inc(res_ready, 1)

            with pool.Fori(0, B) as img:
                prepare_strip(img, 0, "first")
                prepare_strip(img, 1, "second")
                with pool.Fori(1, ROWS - 1) as s:
                    row(img, s)
                    prepare_strip(img, s + 1, "inner")
                row(img, ROWS - 1)
                prepare_strip(img, ROWS, "last")
                row(img, ROWS)

        @block.scalar
        def _(act):
            e = nc.scalar
            for n, name in enumerate("qkvo"):
                act.wait_ge(weights_in, 16 * (n + 1))
                e.activation(w_hi[name][:, :, :], w32[:, 0:KC * C].rearrange("p (k c) -> p k c", k=KC),
                             ACT.Copy, scale=WS).then_inc(split_hi, 1)
            act.wait_ge(weights_in, 16 * 5)
            e.activation(rel_hi[:, :, :], w32[:, :].rearrange("p (n c) -> p n c", n=NREL),
                         ACT.Copy, scale=WS).then_inc(split_hi, 1)
            act.wait_ge(zeroed, NZERO)

            def k_fill(F, i):
                g, n = divmod(i, 2)
                act.wait_ge(fill_done, F + i + 2)
                for half in range(2):
                    r = slice(64 * half, 64 * half + 64)
                    done = e.activation(k_hi[r, 2 * g + half, HALO + 64 * n:HALO + 64 * n + 64, WIN - BLK:WIN],
                                        ps_p[i % 2][r, :].rearrange("p (c r) -> p c r", r=BLK),
                                        ACT.Copy, scale=SCALE / WS)
                done.then_inc(fill_hi, 1)

            def plain_fill(F, i, to, rows=P, cols=512):
                act.wait_ge(fill_done, F + 2)
                e.activation(to, ps_p[i % 2][0:rows, 0:cols], ACT.Copy, scale=1.0 / WS).then_inc(fill_hi, 1)

            def produce(img, s):
                F = fills_before(img, s)
                for i in range(FILLS_Q):
                    plain_fill(F + i, i, q_hi[:, i % 2, i // 2, :])
                act.wait_ge(k_down, img * ROWS + s)
                for i in range(FILLS_K):
                    k_fill(F + FILLS_Q, i)
                F += FILLS_Q + FILLS_K
                with act.Fori(0, 4) as v:
                    for i in range(2):
                        plain_fill(F + 2 * v + i, i, v_hi[:, bass.ds(4 * v + 2 * i, 2), :]
                                   .rearrange("p a c -> p (a c)"), CHUNK)
                plain_fill(F + 8, 0, v_hi[:, CHUNKS - 1, :], CHUNK, C)
                F += FILLS_V
                for i in range(FILLS_B):
                    plain_fill(F + i, i + 1, b_hi[:, i % 2, i // 2, :])

            def exps(U, k):
                act.wait_ge(max_ready, U + 1)
                act.wait_ge(probT_ready, U + 1)
                act.wait_ge(rinv_done, U + 1)
                for j in range(2):
                    done = e.activation(prob[:, k % 2, j, 0:NKEY], ps_s[k % 2][:, j * NKEY:(j + 1) * NKEY],
                                        ACT.Exp, bias=negmax[:, k, j:j + 1], accum_out=rowsum[:, k, j:j + 1])
                done.then_inc(exp_done, 1)

            def probs_hi(U, k):
                act.wait_ge(probT_ready, U + 3)
                act.wait_ge(context_done, U + 1)
                e.activation(pt_hi[:, k % 2, :], ps_t[k % 2][0:CHUNK, :], ACT.Copy).then_inc(pt_hi_done, 1)

            def context_hi(I):
                act.wait_ge(ctxT_ready, I + 2)
                act.wait_ge(fc_done, I + 1)
                e.activation(ct_hi[:, :, :, :], ps_f[:, 0:256].rearrange("p (a h q) -> p a h q", a=2, h=2),
                             ACT.Copy).then_inc(ct_hi_done, 1)

            def turn(I, first, last):
                for k in range(4):
                    U = 4 * I + k
                    if k < 3 or not last:
                        exps(U + 1, (k + 1) % 4)
                    probs_hi(U, k)
                    if k == 1 and not first:
                        context_hi(I - 1)

            with act.Fori(0, B) as img:
                for i in range(FILLS_K):
                    k_fill(img * IMG_FILLS, i)
                with act.Fori(1, ROWS + 1) as s:
                    produce(img, s)
                    I = (img * ROWS + s - 1) * TURNS
                    exps(4 * I, 0)
                    turn(I, True, False)
                    with act.Fori(1, TURNS - 1) as t:
                        turn(I + t, False, False)
                    turn(I + TURNS - 1, False, True)
                    context_hi(I + TURNS - 1)

        @block.vector
        def _(dve):
            e = nc.vector
            for n, name in enumerate("qkvo"):
                dve.wait_ge(split_hi, n + 1)
                e.scalar_tensor_tensor(out=w_lo[name][:, :, :],
                                       in0=w32[:, 0:KC * C].rearrange("p (k c) -> p k c", k=KC), scalar=WS,
                                       in1=w_hi[name][:, :, :], op0=ALU.mult, op1=ALU.subtract)\
                    .then_inc(split_lo, 1)
            dve.wait_ge(split_hi, 5)
            e.scalar_tensor_tensor(out=rel_lo[:, :, :], in0=w32[:, :].rearrange("p (n c) -> p n c", n=NREL),
                                   scalar=WS, in1=rel_hi[:, :, :], op0=ALU.mult, op1=ALU.subtract)\
                .then_inc(split_lo, 1)
            dve.wait_ge(zeroed, NZERO)

            def stats_piece(r, t):
                n = KC * PIX // TURNS
                e.bn_stats(stats[:, bass.ds(r, 1), bass.ds(t, 1), :].rearrange("p a b n -> p (a b n)"),
                           st_load[:, bass.ds(t * n, n)]).then_inc(st_read, 1)

            with dve.Fori(0, ROWS) as r:
                dve.wait_ge(st_in, (r + 1) * 16)
                for t in range(TURNS):
                    stats_piece(r, t)

            def group_stats(img):
                dve.wait_ge(st_read, (img + 1) * ROWS * TURNS + 1)
                dve.sem_inc(dve_went_on, 1)
                for k in range(KC):
                    done = e.bn_aggr(agg[:, k, :], stats[:, :, 4 * k:4 * k + 4, :].rearrange("p r t n -> p r (t n)"))
                done.then_inc(gn_step, 1)
                dve.wait_ge(gn_mean, 2 * img + 1)
                e.tensor_copy(mean_sb[:, :], ps_p[0][:, 0:KC]).then_inc(gn_step, 1)
                dve.wait_ge(gn_step, 6 * img + 2)
                e.tensor_tensor(gn[:, 0, :], agg[:, :, 0], mean_sb[:, :], ALU.subtract).then_inc(gn_step, 1)
                dve.wait_ge(gn_step, 6 * img + 3)
                e.tensor_tensor(gn[:, 1, :], gn[:, 0, :], gn[:, 0, :], ALU.mult).then_inc(gn_step, 1)
                dve.wait_ge(gn_step, 6 * img + 4)
                e.tensor_tensor(gn[:, 2, :], gn[:, 1, :], agg[:, :, 1], ALU.add).then_inc(gn_step, 1)
                dve.wait_ge(gn_mean, 2 * img + 2)
                e.tensor_scalar(gn[:, 3, :], ps_p[0][:, KC:2 * KC], GN_EPS, None, ALU.add).then_inc(gn_step, 1)

            def k_fill(F, i):
                g, n = divmod(i, 2)
                dve.wait_ge(fill_hi, F + i + 1)
                for half in range(2):
                    r = slice(64 * half, 64 * half + 64)
                    at = (r, 2 * g + half, slice(HALO + 64 * n, HALO + 64 * n + 64), slice(WIN - BLK, WIN))
                    done = e.scalar_tensor_tensor(out=k_lo[at],
                                                  in0=ps_p[i % 2][r, :].rearrange("p (c r) -> p c r", r=BLK),
                                                  scalar=SCALE / WS, in1=k_hi[at],
                                                  op0=ALU.mult, op1=ALU.subtract)
                done.then_inc(fill_lo, 1)

            def plain_fill(F, i, to, high, rows=P, cols=512):
                dve.wait_ge(fill_hi, F + 1)
                e.scalar_tensor_tensor(out=to, in0=ps_p[i % 2][0:rows, 0:cols], scalar=1.0 / WS, in1=high,
                                       op0=ALU.mult, op1=ALU.subtract).then_inc(fill_lo, 1)

            def produce(img, s):
                F = fills_before(img, s)
                for i in range(FILLS_Q):
                    plain_fill(F + i, i, q_lo[:, i % 2, i // 2, :], q_hi[:, i % 2, i // 2, :])
                    if i == 0:
                        dve.wait_ge(fill_hi, F)
                        dve.wait_ge(fill_lo, F + 2)
                        for half in range(2):
                            r = slice(64 * half, 64 * half + 64)
                            for kk in (k_hi, k_lo):
                                done = e.tensor_copy(kk[r, half::2, :, 0:WIN - BLK], kk[r, half::2, :, BLK:WIN])
                        done.then_inc(k_down, 1)
                dve.wait_ge(k_down, img * ROWS + s)
                for i in range(FILLS_K):
                    k_fill(F + FILLS_Q, i)
                F += FILLS_Q + FILLS_K
                with dve.Fori(0, 4) as v:
                    for i in range(2):
                        at = bass.ds(4 * v + 2 * i, 2)
                        plain_fill(F + 2 * v + i, i, v_lo[:, at, :].rearrange("p a c -> p (a c)"),
                                   v_hi[:, at, :].rearrange("p a c -> p (a c)"), CHUNK)
                plain_fill(F + 8, 0, v_lo[:, CHUNKS - 1, :], v_hi[:, CHUNKS - 1, :], CHUNK, C)
                F += FILLS_V
                for i in range(FILLS_B):
                    plain_fill(F + i, i + 1, b_lo[:, i % 2, i // 2, :], b_hi[:, i % 2, i // 2, :])
                    if i % 2 == 1:
                        par = i // 2
                        dve.wait_ge(fill_lo, F + i + 1 + 2)
                        for m in range(4):
                            hq = (m + 2) % 4
                            r = slice(32 * m, 32 * m + 32)
                            for to, frm in ((qd_hi, b_hi), (qd_lo, b_lo)):
                                done = e.tensor_copy(to[r, hq // 2::2, par, :, hq % 2, :],
                                                     frm[r, :, par, :].rearrange("p g (t q) -> p g t q", q=NQ))
                        done.then_inc(bd_ready, 1)

            def maxima(U, k):
                dve.wait_ge(scores_ready, U + 1)
                e.tensor_reduce(negmax[:, k, :], ps_s[k % 2][:, 0:2 * NKEY].rearrange("p (j n) -> p j n", j=2),
                                AX.X, ALU.max, negate=True).then_inc(max_ready, 1)

            def probs_lo(U, k):
                dve.wait_ge(pt_hi_done, U + 1)
                e.tensor_tensor(pt_lo[:, k % 2, :], ps_t[k % 2][0:CHUNK, :], pt_hi[:, k % 2, :],
                                ALU.subtract).then_inc(pt_lo_done, 1)

            def reciprocals(U, k):
                dve.wait_ge(exp_done, U + 3)
                e.reciprocal(rinv[:, k, :], rowsum[:, k, :]).then_inc(rinv_done, 1)

            def normalise(I):
                dve.wait_ge(context_done, 4 * I + 4 + 2)
                dve.wait_ge(rinv_done, 4 * I + 4 + 4)
                dve.wait_ge(ctxT_ready, I + 1)
                for half in range(2):
                    r = slice(64 * half, 64 * half + 64)
                    done = e.tensor_tensor(ctxn[r, :, :, :].rearrange("p a b d -> p (a b) d"),
                                           ps_c[r, :].rearrange("p (u d) -> p u d", d=2 * DH)
                                           [:, :, DH * half:DH * half + DH],
                                           rinv[r, :, :].rearrange("p k j -> p (k j)").unsqueeze(2)
                                           .broadcast_to([64, 2 * PAIRS, DH]), ALU.mult)
                done.then_inc(norm_done, 1)

            def context_lo(I):
                dve.wait_ge(ct_hi_done, I + 1)
                e.tensor_tensor(ct_lo[:, :, :, :], ps_f[:, 0:256].rearrange("p (a h q) -> p a h q", a=2, h=2),
                                ct_hi[:, :, :, :], ALU.subtract).then_inc(ct_lo_done, 1)

            def add_output(I, t):
                dve.wait_ge(fc_done, I + 2)
                at = res[:, :, :, bass.ds(t * 2 * BLK, 2 * BLK)].rearrange("p k x c -> p (k x) c")
                e.scalar_tensor_tensor(out=at, in0=ps_f[:, 256:512].rearrange("p (m c) -> p m c", c=2 * BLK),
                                       scalar=1.0 / WS, in1=at, op0=ALU.mult, op1=ALU.add)\
                    .then_inc(out_added, 1)

            def turn(I, t, r, first, last):
                for k in range(4):
                    U = 4 * I + k
                    if k < 3 or not last:
                        maxima(U + 1, (k + 1) % 4)
                    probs_lo(U, k)
                    if k == 0 and not first:
                        normalise(I - 1)
                    if k == 0:
                        dve.wait_ge(norm_done, I + 1)
                    if k == 1 and not first:
                        context_lo(I - 1)
                    if k == 3 and not first:
                        add_output(I - 1, t - 1)
                    reciprocals(U, k)
                    if k == 2:
                        stats_piece(r, t)

            with dve.Fori(0, B) as img:
                group_stats(img)
                for i in range(FILLS_K):
                    k_fill(img * IMG_FILLS, i)
                with dve.Fori(1, ROWS + 1) as s:
                    produce(img, s)
                    rr = img * ROWS + s - 1
                    I = rr * TURNS
                    dve.wait_ge(res_ready, rr + 1)
                    dve.wait_ge(st_in, (ROWS + rr + 1) * 16)
                    maxima(4 * I, 0)
                    turn(I, 0, s - 1, True, False)
                    with dve.Fori(1, TURNS - 1) as t:
                        turn(I + t, t, s - 1, False, False)
                    turn(I + TURNS - 1, TURNS - 1, s - 1, False, True)
                    normalise(I + TURNS - 1)
                    context_lo(I + TURNS - 1)
                    add_output(I + TURNS - 1, TURNS - 1)

        @block.tensor
        def _(pe):
            mm = nc.tensor.matmul
            pe.wait_ge(consts_in, 48)
            pe.wait_ge(zeroed, NZERO)
            pe.wait_ge(split_lo, 5)
            pe.wait_ge(onehot_in, 16 * PAIRS)

            def group_stats(img):
                pe.wait_ge(fill_lo, img * IMG_FILLS + 2)
                pe.wait_ge(gn_step, 6 * img + 1)
                mm(ps_p[0][:, 0:KC], gmean[:, :], agg[:, :, 0], start=True, stop=True).then_inc(gn_mean, 1)
                pe.wait_ge(gn_step, 6 * img + 5)
                mm(ps_p[0][:, KC:2 * KC], gmean[:, :], gn[:, 2, :], start=True, stop=True).then_inc(gn_mean, 1)

            def three(out_ap, terms, first=True, last=True):
                n = 3 * len(terms)
                i = 0
                for wh, wl, xh, xl in terms:
                    for a, b in ((wh, xh), (wh, xl), (wl, xh)):
                        done = mm(out_ap, a, b, start=first and i == 0, stop=last and i == n - 1,
                                  skip_group_check=True)
                        i += 1
                return done

            def bank_free(F, first):
                pe.wait_ge(fill_lo, F + (2 if first else 1))

            def k_fill(F, i):
                g, n = divmod(i, 2)
                bank_free(F + i, i == 0)
                cols = slice(HALO + 64 * n, HALO + 64 * n + 64)
                three(ps_p[i % 2][:, :],
                      [(w_hi["k"][:, k, g * P:(g + 1) * P], w_lo["k"][:, k, g * P:(g + 1) * P],
                        xn_hi[:, k, cols, WIN - BLK:WIN], xn_lo[:, k, cols, WIN - BLK:WIN])
                       for k in range(KC)]).then_inc(fill_done, 1)

            def q_fill(F, i):
                par, g = divmod(i, 2)
                bank_free(F + i, i == 0)

                def tokens(xn, k):
                    inside = xn[:, k, HALO:HALO + W, HALO:HALO + BLK]
                    return inside.rearrange("p (t a c) r -> p t a c r", a=2, c=BLK)[:, :, par, :, :]

                three(ps_p[i % 2][:, :],
                      [(w_hi["q"][:, k, g * P:(g + 1) * P], w_lo["q"][:, k, g * P:(g + 1) * P],
                        tokens(xn_hi, k), tokens(xn_lo, k)) for k in range(KC)]).then_inc(fill_done, 1)

            def v_fill(F, i, chunks):
                pe.wait_ge(fill_lo, F + 1)
                for j, c in enumerate(chunks):
                    for n, (k, a, b) in enumerate([(k, a, b) for k in range(KC)
                                                   for a, b in ((0, 0), (0, 1), (1, 0))]):
                        src = ((xn_hi, xn_lo)[a])[:, k, :, :].rearrange("p c r -> p (c r)")
                        done = mm(ps_p[i % 2][0:CHUNK, j * C:(j + 1) * C],
                                  src[:, bass.ds(c * CHUNK, CHUNK)],
                                  (w_hi, w_lo)[b]["v"][:, k, :], start=n == 0, stop=n == 5,
                                  skip_group_check=True)
                done.then_inc(fill_done, 1)

            def b_fill(F, i, bank):
                par, g = divmod(i, 2)
                bank_free(F, False)
                acc = ps_p[bank][:, :].rearrange("p (t y x) -> p t y x", y=BLK, x=BLK)
                qh = q_hi[:, g, par, :].rearrange("p (t y x) -> p t y x", y=BLK, x=BLK)
                ql = q_lo[:, g, par, :].rearrange("p (t y x) -> p t y x", y=BLK, x=BLK)
                for y in range(BLK):
                    n = par * BLK + y
                    three(acc[:, :, y, :], [(rel_hi[:, n, :], rel_lo[:, n, :], qh[:, :, y, :], ql[:, :, y, :])],
                          first=y == 0, last=False)
                for xx in range(BLK):
                    n = 2 * BLK + xx
                    done = three(acc[:, :, :, xx], [(rel_hi[:, n, :], rel_lo[:, n, :],
                                                     qh[:, :, :, xx], ql[:, :, :, xx])],
                                 first=False, last=xx == BLK - 1)
                done.then_inc(fill_done, 1)

            def produce(img, s):
                F = fills_before(img, s)
                pe.wait_ge(xn_ready, img * (ROWS + 1) + s + 1)
                for i in range(FILLS_Q):
                    q_fill(F, i)
                for i in range(FILLS_K):
                    k_fill(F + FILLS_Q, i)
                F += FILLS_Q + FILLS_K
                with pe.Fori(0, 4) as v:
                    for i in range(2):
                        v_fill(F + 2 * v + i, i, (4 * v + 2 * i, 4 * v + 2 * i + 1))
                v_fill(F + 8, 0, (CHUNKS - 1,))
                F += FILLS_V
                for i in range(FILLS_B):
                    b_fill(F + i, i, (i + 1) % 2)

            def scores(U, k, t):
                par, g = divmod(k, 2)
                pe.wait_ge(exp_done, U + 1)
                for j in range(2):
                    p = 2 * g + j

                    def queries(qd):
                        return qd[:, p, par, :, :, :].rearrange("p t h q -> p (t h q)")[
                            :, bass.ds(t * 2 * NQ, 2 * NQ)]

                    def keys(kk):
                        return kk[:, p, :, :].rearrange("p c r -> p (c r)")[
                            :, bass.ds((2 * t + par) * CHUNK, NKEY)]

                    done = three(ps_s[k % 2][:, j * NKEY:(j + 1) * NKEY],
                                 [(queries(qd_hi), queries(qd_lo), keys(k_hi), keys(k_lo))])
                done.then_inc(scores_ready, 1)

            def transpose_probs(U, k):
                pe.wait_ge(exp_done, U + 3)
                pe.wait_ge(pt_lo_done, U + 1)
                for j in range(2):
                    for c in range(2):
                        at = (2 * j + c) * P
                        done = nc.tensor.transpose(ps_t[k % 2][0:CHUNK, at:at + P],
                                                   prob[:, k % 2, j, c * CHUNK:(c + 1) * CHUNK], ident[:, :])
                done.then_inc(probT_ready, 1)

            def context(U, k, t, I):
                par, g = divmod(k, 2)
                pe.wait_ge(pt_lo_done, U + 3)
                if k == 0:
                    pe.wait_ge(norm_done, I + 1)
                for j in range(2):
                    p = 2 * g + j
                    terms = []
                    for c in range(2):
                        at = (2 * j + c) * P

                        def values(v):
                            return v[:, bass.ds(2 * t + par + c, 1), p * 2 * DH:(p + 1) * 2 * DH]\
                                .rearrange("p a c -> p (a c)")

                        terms.append((pt_hi[:, k % 2, at:at + P], pt_lo[:, k % 2, at:at + P],
                                      values(v_hi), values(v_lo)))
                    at = (par * PAIRS + p) * 2 * DH
                    done = three(ps_c[:, at:at + 2 * DH], terms)
                done.then_inc(context_done, 1)

            def transpose_context(I):
                pe.wait_ge(norm_done, I + 2)
                pe.wait_ge(out_added, I + 1)
                for par in range(2):
                    done = nc.tensor.transpose(ps_f[:, par * P:(par + 1) * P],
                                               ctxn[:, par, :, :].rearrange("p a d -> p (a d)"), ident[:, :])
                done.then_inc(ctxT_ready, 1)

            def output(I):
                pe.wait_ge(ct_lo_done, I + 1)

                def tokens(ct, half):
                    return ct[:, :, half, :].rearrange("p a (y x) -> p x a y", y=BLK)

                for k in range(KC):
                    done = three(ps_f[:, 256 + k * P:256 + (k + 1) * P],
                                 [(w_hi["o"][:, half, k * P:(k + 1) * P], w_lo["o"][:, half, k * P:(k + 1) * P],
                                   tokens(ct_hi, half), tokens(ct_lo, half)) for half in range(2)])
                done.then_inc(fc_done, 1)

            def turn(I, t, first, last):
                for k in range(4):
                    U = 4 * I + k
                    if k < 3:
                        scores(U + 1, k + 1, t)
                    elif not last:
                        scores(U + 1, 0, t + 1)
                    transpose_probs(U, k)
                    if k == 1 and not first:
                        transpose_context(I - 1)
                    if k > 0:
                        context(U - 1, k - 1, t, I)
                    elif not first:
                        context(U - 1, 3, t - 1, I - 1)
                    if k == 2 and not first:
                        output(I - 1)

            with pe.Fori(0, B) as img:
                group_stats(img)
                pe.wait_ge(xn_ready, img * (ROWS + 1) + 1)
                for i in range(FILLS_K):
                    k_fill(img * IMG_FILLS, i)
                with pe.Fori(1, ROWS + 1) as s:
                    produce(img, s)
                    rr = img * ROWS + s - 1
                    I = rr * TURNS
                    pe.wait_ge(qd_ready, 2 * rr + 1)
                    pe.wait_ge(bd_ready, 2 * rr + 1)
                    scores(4 * I, 0, 0)
                    pe.wait_ge(qd_ready, 2 * rr + 2)
                    pe.wait_ge(bd_ready, 2 * rr + 2)
                    turn(I, 0, True, False)
                    with pe.Fori(1, TURNS - 1) as t:
                        turn(I + t, t, False, False)
                    turn(I + TURNS - 1, TURNS - 1, False, True)
                    context(4 * I + 4 * TURNS - 1, 3, TURNS - 1, I + TURNS - 1)
                    transpose_context(I + TURNS - 1)
                    output(I + TURNS - 1)


def _relative_weights(np, rel_w, rel_h):
    full = np.zeros((P, NREL, P), np.float32)
    for m in range(4):
        hq = (m + 2) % 4
        rows = slice(DH * hq, DH * hq + DH)
        for n in range(NREL):
            q = n % BLK
            for j in range(WIN):
                if n < 2 * BLK:
                    full[rows, n, 32 * m + (j + BLK * (n // BLK)) % 16] = rel_w[j - q + WIN - 1]
                else:
                    full[rows, n, 32 * m + 16 + j] = rel_h[j - q + WIN - 1]
    return full.reshape(P, NREL * P)


def kernel(**inputs):
    import numpy as _np
    import concourse.bacc as _bacc
    from concourse import mybir as _mybir
    from concourse.bass_utils import run_bass_kernel_spmd as _run

    a = {n: _np.asarray(v) for n, v in inputs.items()}
    x, w_q, w_kv = a["x"], a["L0_conv_w_q"], a["L0_conv_w_kv"]
    fc_w, fc_b = a["L0_conv_fc_w"], a["L0_conv_fc_b"]

    def halves(w):
        return w.T.reshape(KC, P, C).transpose(1, 0, 2).reshape(P, KC * C)

    fc = fc_w.T.reshape(PAIRS, 2, DH, C).transpose(1, 0, 2, 3).reshape(KC, P, C)
    col, row = _np.arange(WP)[:, None], _np.arange(WIN)[None, :]
    onehot = _np.zeros((P, WP, WIN), _np.float16)
    for m in range(4):
        for r in range(16):
            onehot[32 * m + r] = (col % 16 == r) & (row >= 0)
        for i in range(WIN):
            onehot[32 * m + 16 + i] = (row == i) & (col >= 0)
    gmean = _np.kron(_np.eye(P // CG), _np.full((CG, CG), 1.0 / CG)).astype(_np.float32)
    arrays = {
        "x": x, "wqT": halves(w_q), "wkT": halves(w_kv[:C]), "wvT": halves(w_kv[C:]),
        "fcT": fc.transpose(1, 0, 2).reshape(P, KC * C), "fcb": fc_b.reshape(KC, P).T,
        "rel": _relative_weights(_np, a["L0_conv_rel_w"], a["L0_conv_rel_h"]), "onehot": onehot,
        "ident": _np.eye(P, dtype=_np.float32), "gmean": gmean,
    }
    arrays = {n: _np.ascontiguousarray(v) for n, v in arrays.items()}
    nc = _bacc.Bacc("TRN2", target_bir_lowering=False, num_devices=1)
    args = [nc.dram_tensor(f"in_{n}", v.shape, _mybir.dt.from_np(v.dtype), kind="ExternalInput").ap()
            for n, v in arrays.items()]
    args.append(nc.dram_tensor("out_0", x.shape, _mybir.dt.float32, kind="ExternalOutput").ap())
    halo_attention_program(nc, *args)
    r = _run(nc, [{f"in_{n}": v for n, v in arrays.items()}], core_ids=[0])
    return r.results[0]["out_0"]
```

```python
from contextlib import ExitStack

import concourse.bass as bass
from concourse import mybir

F32 = mybir.dt.float32
F16 = mybir.dt.float16
ALU = mybir.AluOpType
ACT = mybir.ActivationFunctionType
AX = mybir.AxisListType

P = 128
C, H, W = 256, 128, 128
HEADS, DH = 8, 32
BLK, HALO = 8, 3
WIN = BLK + 2 * HALO
NKEY = WIN * WIN
NQ = BLK * BLK
GROUPS, GN_EPS = 32, 1e-5
CG = C // GROUPS
KC = C // P
ROWS = H // BLK
TURNS = W // BLK // 2
WP = W + BLK
CHUNK = BLK * WIN
CHUNKS = WP // BLK
PADK = 2 * CHUNK
PAIRS = HEADS // 2
PIX = BLK * W
NREL = 3 * BLK
WS = 64.0
SCALE = float(DH) ** -0.5
FILLS_Q, FILLS_K, FILLS_V, FILLS_B = 4, 4, 9, 4
FILLS = FILLS_Q + FILLS_K + FILLS_V + FILLS_B
NWORD = 6


def halo_attention_program(nc, x, wqT, wkT, wvT, fcT, fcb, rel, onehot, ident_in, gmean_in, out):
    B = x.shape[0]
    IMG_FILLS = FILLS_K + ROWS * FILLS

    with ExitStack() as ctx:
        def sb(name, shape, dt):
            return ctx.enter_context(nc.sbuf_tensor(name, shape, dt))

        def psum(name):
            return ctx.enter_context(nc.psum_tensor(name, [P, 512], F32))

        def sem(name):
            return ctx.enter_context(nc.semaphore(name))

        ident = sb("ident", [P, P], F32)
        gmean = sb("gmean", [P, P], F32)
        w32 = sb("w32", [P, NREL * P], F32)
        w_hi = {n: sb(f"w{n}_hi", [P, KC, C], F16) for n in "qkvo"}
        w_lo = {n: sb(f"w{n}_lo", [P, KC, C], F16) for n in "qkvo"}
        rel_hi = sb("rel_hi", [P, NREL, P], F16)
        rel_lo = sb("rel_lo", [P, NREL, P], F16)
        fcb_sb = sb("fcb_sb", [P, KC], F32)
        x_load = sb("x_load", [P, KC, BLK, W], F32)
        x_norm = sb("x_norm", [P, KC, BLK, W], F32)
        st_load = sb("st_load", [P, KC * PIX], F32)
        stats = sb("stats", [P, ROWS, TURNS, NWORD], F32)
        gn = sb("gn", [P, 8, KC], F32)
        agg = sb("agg", [P, KC, 2], F32)
        mean_sb = sb("mean_sb", [P, KC], F32)
        rstd_sb = sb("rstd_sb", [P, KC], F32)
        xn_hi = sb("xn_hi", [P, KC, WP, WIN], F16)
        xn_lo = sb("xn_lo", [P, KC, WP, WIN], F16)
        k_hi = sb("k_hi", [P, PAIRS, WP, WIN], F16)
        k_lo = sb("k_lo", [P, PAIRS, WP, WIN], F16)
        q_hi = sb("q_hi", [P, 2, 2, TURNS * NQ], F16)
        q_lo = sb("q_lo", [P, 2, 2, TURNS * NQ], F16)
        b_hi = sb("b_hi", [P, 2, 2, TURNS * NQ], F16)
        b_lo = sb("b_lo", [P, 2, 2, TURNS * NQ], F16)
        qd_hi = sb("qd_hi", [P, PAIRS, 2, TURNS, 2, NQ], F16)
        qd_lo = sb("qd_lo", [P, PAIRS, 2, TURNS, 2, NQ], F16)
        v_hi = sb("v_hi", [CHUNK, CHUNKS, C], F16)
        v_lo = sb("v_lo", [CHUNK, CHUNKS, C], F16)
        negmax = sb("negmax", [P, 4, 2], F32)
        rowsum = sb("rowsum", [P, 4, 2], F32)
        rinv = sb("rinv", [P, 4, 2], F32)
        prob = sb("prob", [P, 2, 2, PADK], F32)
        pt_hi = sb("pt_hi", [CHUNK, 2, 512], F16)
        pt_lo = sb("pt_lo", [CHUNK, 2, 512], F16)
        ctxn = sb("ctxn", [P, 2, PAIRS, DH], F32)
        ct_hi = sb("ct_hi", [P, 2, 2, NQ], F16)
        ct_lo = sb("ct_lo", [P, 2, 2, NQ], F16)
        res = sb("res", [P, KC, BLK, W], F32)

        ps_s = [psum(f"ps_scores{i}") for i in range(2)]
        ps_t = [psum(f"ps_probT{i}") for i in range(2)]
        ps_c = psum("ps_context")
        ps_f = psum("ps_output")
        ps_p = [psum(f"ps_project{i}") for i in range(2)]

        weights_in = sem("weights_in")
        consts_in = sem("consts_in")
        split_hi = sem("split_hi")
        split_lo = sem("split_lo")
        zeroed = sem("zeroed")
        onehot_in = sem("onehot_in")
        st_in = sem("st_in")
        st_read = sem("st_read")
        gn_step = sem("gn_step")
        gn_mean = sem("gn_mean")
        gn_ready = sem("gn_ready")
        x_in = sem("x_in")
        x_read = sem("x_read")
        pool_step = sem("pool_step")
        xn_ready = sem("xn_ready")
        res_in = sem("res_in")
        res_ready = sem("res_ready")
        out_stored = sem("out_stored")
        pool_went_on = sem("pool_went_on")
        dve_went_on = sem("dve_went_on")
        fill_done = sem("fill_done")
        fill_hi = sem("fill_hi")
        fill_lo = sem("fill_lo")
        k_down = sem("k_down")
        qd_hi_ready = sem("qd_hi_ready")
        qd_lo_ready = sem("qd_lo_ready")
        bd_ready = sem("bd_ready")
        scores_ready = sem("scores_ready")
        max_ready = sem("max_ready")
        exp_done = sem("exp_done")
        rinv_done = sem("rinv_done")
        probT_ready = sem("probT_ready")
        pt_hi_done = sem("pt_hi_done")
        pt_lo_done = sem("pt_lo_done")
        context_done = sem("context_done")
        norm_done = sem("norm_done")
        ctxT_ready = sem("ctxT_ready")
        ct_hi_done = sem("ct_hi_done")
        ct_lo_done = sem("ct_lo_done")
        fc_done = sem("fc_done")
        out_added = sem("out_added")

        CREDITS = [(exp_done, 2), (probT_ready, 2), (rinv_done, 4), (pt_lo_done, 2), (context_done, 2),
                   (norm_done, 1), (ctxT_ready, 1), (fc_done, 1), (out_added, 1), (fill_done, 1),
                   (fill_lo, 2), (st_read, 1), (x_read, 1), (out_stored, 16)]
        NZERO = 8
        scratch = sb("scratch", [P, len(CREDITS)], F32)
        mhalf = sb("mhalf", [P, KC], F32)

        block = ctx.enter_context(nc.Block())

        def fills_before(img, s):
            return img * IMG_FILLS + FILLS_K + (s - 1) * FILLS

        @block.sync
        def _(sp):
            sp.dma_start(ident[:, :], ident_in).then_inc(consts_in, 16)
            sp.dma_start(gmean[:, :], gmean_in).then_inc(consts_in, 16)
            sp.dma_start(fcb_sb[:, :], fcb).then_inc(consts_in, 16)
            for n, w in enumerate((wqT, wkT, wvT, fcT, rel)):
                if n:
                    sp.wait_ge(split_lo, n)
                sp.dma_start(w32[:, 0:w.shape[1]], w).then_inc(weights_in, 16)
            sp.wait_ge(zeroed, NZERO)
            for p in range(PAIRS):
                r0 = 64 if p % 2 == 0 else 0
                sp.dma_start(k_hi[r0:r0 + 64, p, :, :], onehot[r0:r0 + 64, :, :]).then_inc(onehot_in, 16)

            x_pix = x.rearrange("b (k p) h w -> p b k (h w)", p=P)
            out_pix = out.rearrange("b (k p) h w -> p b k (h w)", p=P)

            def load_stats(img, r, piece):
                sp.wait_ge(st_read, piece * TURNS + 1)
                sp.dma_start(st_load[:, :].rearrange("p (k n) -> p k n", k=KC),
                             x_pix[:, bass.ds(img, 1), :, bass.ds(r * PIX, PIX)]
                             .rearrange("p a k n -> p (a k) n")).then_inc(st_in, 16)

            def load_strip(img, s, first_row, to_row, rows):
                sp.wait_ge(x_read, img * (ROWS + 1) + s + 1)
                for k in range(KC):
                    sp.dma_start(x_load[:, k, to_row:to_row + rows, :].rearrange("p r w -> p (r w)"),
                                 x_pix[:, bass.ds(img, 1), k, bass.ds(first_row * W, rows * W)]
                                 .rearrange("p a n -> p (a n)")).then_inc(x_in, 16)

            def load_residual(img, s):
                sp.wait_ge(out_stored, ((img * ROWS + s - 1) * KC + 1) * 16)
                for k in range(KC):
                    sp.dma_start(res[:, k, :, :].rearrange("p r w -> p (r w)"),
                                 x_pix[:, bass.ds(img, 1), k, bass.ds((s - 1) * PIX, PIX)]
                                 .rearrange("p a n -> p (a n)")).then_inc(res_in, 16)

            def store_row(img, s):
                sp.wait_ge(out_added, (img * ROWS + s) * TURNS + 1)
                for k in range(KC):
                    sp.dma_start(out_pix[:, bass.ds(img, 1), k, bass.ds((s - 1) * PIX, PIX)]
                                 .rearrange("p a n -> p (a n)"),
                                 res[:, k, :, :].rearrange("p r w -> p (r w)")).then_inc(out_stored, 16)

            with sp.Fori(0, ROWS) as r:
                load_stats(0, r, r)
            with sp.Fori(0, B) as img:
                load_strip(img, 0, 0, BLK - HALO, HALO)
                load_strip(img, 1, HALO, 0, BLK)
                with sp.Fori(1, ROWS - 1) as s:
                    load_residual(img, s)
                    load_stats((img + 1) % B, s - 1, (img + 1) * ROWS + s - 1)
                    load_strip(img, s + 1, s * BLK + HALO, 0, BLK)
                    store_row(img, s)
                for s in (ROWS - 1, ROWS):
                    load_residual(img, s)
                    load_stats((img + 1) % B, s - 1, (img + 1) * ROWS + s - 1)
                    if s < ROWS:
                        load_strip(img, s + 1, s * BLK + HALO, 0, BLK - HALO)
                    store_row(img, s)
            sp.wait_ge(out_stored, (B * ROWS * KC + 1) * 16)

        @block.gpsimd
        def _(pool):
            g = nc.gpsimd
            g.memset(k_hi[:, :, :, :], 0.0).then_inc(zeroed, 1)
            g.memset(k_lo[:, :, :, :], 0.0).then_inc(zeroed, 1)
            g.memset(xn_hi[:, :, :, :], 0.0).then_inc(zeroed, 1)
            g.memset(xn_lo[:, :, :, :], 0.0).then_inc(zeroed, 1)
            g.memset(qd_hi[:, :, :, :, :, :], 0.0).then_inc(zeroed, 1)
            g.memset(qd_lo[:, :, :, :, :, :], 0.0).then_inc(zeroed, 1)
            g.memset(prob[:, :, :, :], 0.0).then_inc(zeroed, 1)
            g.memset(mhalf[:, :], -0.5).then_inc(zeroed, 1)
            for at, (s, n) in enumerate(CREDITS):
                g.memset(scratch[:, at:at + 1], 0.0).then_inc(s, n)
            pool.wait_ge(zeroed, NZERO)
            pool.wait_ge(consts_in, 48)

            inner = slice(HALO, HALO + W)
            keep = WIN - BLK

            def prepare_strip(img, s, kind):
                n = img * (ROWS + 1) + s
                if kind == "first":
                    pool.wait_ge(fill_done, img * IMG_FILLS + 1)
                    pool.sem_inc(pool_went_on, 1)
                    g.memset(xn_hi[:, :, :, keep:WIN - HALO], 0.0)
                    g.memset(xn_lo[:, :, :, keep:WIN - HALO], 0.0).then_inc(pool_step, 2)
                    pool.wait_ge(gn_step, 6 * img + 6)
                    pool.sem_inc(pool_went_on, 1)
                    g.tensor_tensor(rstd_sb[:, :], gn[:, 3, :], mhalf[:, :], ALU.pow).then_inc(gn_ready, 1)
                    pool.wait_ge(gn_ready, img + 1)
                    pool.sem_inc(pool_went_on, 1)
                    at, rows, frm = WIN - HALO, HALO, BLK - HALO
                else:
                    read = img * IMG_FILLS + FILLS_K if kind == "second" else \
                        fills_before(img, s - 1) + FILLS
                    pool.wait_ge(fill_done, read + 1)
                    pool.sem_inc(pool_went_on, 1)
                    g.tensor_scalar(xn_hi[:, :, :, 0:keep], xn_hi[:, :, :, BLK:WIN], 1.0, None, ALU.mult)
                    copied = g.tensor_scalar(xn_lo[:, :, :, 0:keep], xn_lo[:, :, :, BLK:WIN], 1.0, None,
                                             ALU.mult)
                    at, rows, frm = keep, BLK, 0
                    if kind == "last":
                        copied.then_inc(pool_step, 1)
                        pool.wait_ge(pool_step, 3 * n + 1)
                        pool.sem_inc(pool_went_on, 1)
                        rows = BLK - HALO
                        g.memset(xn_hi[:, :, :, WIN - HALO:WIN], 0.0)
                        g.memset(xn_lo[:, :, :, WIN - HALO:WIN], 0.0).then_inc(pool_step, 1)
                    else:
                        copied.then_inc(pool_step, 2)
                pool.wait_ge(x_in, (n + 1) * KC * 16)
                pool.sem_inc(pool_went_on, 1)
                for k in range(KC):
                    done = g.tensor_scalar(x_norm[:, k, frm:frm + rows, :], x_load[:, k, frm:frm + rows, :],
                                           mean_sb[:, k:k + 1], rstd_sb[:, k:k + 1],
                                           ALU.subtract, ALU.mult)
                done.then_inc(x_read, 1)
                pool.wait_ge(x_read, n + 2)
                pool.wait_ge(pool_step, 3 * n + 2)
                pool.sem_inc(pool_went_on, 1)
                columns = x_norm[:, :, frm:frm + rows, :].rearrange("p k r w -> p k w r")
                for k in range(KC):
                    done = g.tensor_scalar(xn_hi[:, k, inner, at:at + rows], columns[:, k, :, :], 1.0, None,
                                           ALU.mult)
                done.then_inc(pool_step, 1)
                pool.wait_ge(pool_step, 3 * n + 3)
                pool.sem_inc(pool_went_on, 1)
                for k in range(KC):
                    done = g.tensor_tensor(xn_lo[:, k, inner, at:at + rows], columns[:, k, :, :],
                                           xn_hi[:, k, inner, at:at + rows], ALU.subtract)
                done.then_inc(xn_ready, 1)

            def row(img, s):
                rr = img * ROWS + s - 1
                pool.wait_ge(res_in, (rr + 1) * KC * 16)
                pool.sem_inc(pool_went_on, 1)
                for k in range(KC):
                    done = g.tensor_scalar(res[:, k, :, :], res[:, k, :, :], fcb_sb[:, k:k + 1], None, ALU.add)
                done.then_inc(res_ready, 1)

            with pool.Fori(0, B) as img:
                prepare_strip(img, 0, "first")
                prepare_strip(img, 1, "second")
                with pool.Fori(1, ROWS - 1) as s:
                    row(img, s)
                    prepare_strip(img, s + 1, "inner")
                row(img, ROWS - 1)
                prepare_strip(img, ROWS, "last")
                row(img, ROWS)

        @block.scalar
        def _(act):
            e = nc.scalar
            for n, name in enumerate("qkvo"):
                act.wait_ge(weights_in, 16 * (n + 1))
                e.activation(w_hi[name][:, :, :], w32[:, 0:KC * C].rearrange("p (k c) -> p k c", k=KC),
                             ACT.Copy, scale=WS).then_inc(split_hi, 1)
            act.wait_ge(weights_in, 16 * 5)
            e.activation(rel_hi[:, :, :], w32[:, :].rearrange("p (n c) -> p n c", n=NREL),
                         ACT.Copy, scale=WS).then_inc(split_hi, 1)
            act.wait_ge(zeroed, NZERO)

            def k_fill(F, i):
                g, n = divmod(i, 2)
                act.wait_ge(fill_done, F + i + 2)
                for half in range(2):
                    r = slice(64 * half, 64 * half + 64)
                    done = e.activation(k_hi[r, 2 * g + half, HALO + 64 * n:HALO + 64 * n + 64, WIN - BLK:WIN],
                                        ps_p[i % 2][r, :].rearrange("p (c r) -> p c r", r=BLK),
                                        ACT.Copy, scale=SCALE / WS)
                done.then_inc(fill_hi, 1)

            def plain_fill(F, i, to, rows=P, cols=512):
                act.wait_ge(fill_done, F + 2)
                e.activation(to, ps_p[i % 2][0:rows, 0:cols], ACT.Copy, scale=1.0 / WS).then_inc(fill_hi, 1)

            def place_queries(par, hq):
                r = slice(32 * hq, 32 * hq + 32)
                return e.activation(qd_hi[r, hq // 2::2, par, :, hq % 2, :],
                                    q_hi[r, :, par, :].rearrange("p g (t q) -> p g t q", q=NQ), ACT.Copy)

            def produce(img, s, tail):
                F = fills_before(img, s)
                for i in range(FILLS_Q):
                    plain_fill(F + i, i, q_hi[:, i % 2, i // 2, :])
                    if tail and i == 1:
                        context_hi((img * ROWS + s - 1) * TURNS - 1)
                act.wait_ge(k_down, img * ROWS + s)
                for i in range(FILLS_K):
                    k_fill(F + FILLS_Q, i)
                act.wait_ge(fill_hi, F + FILLS_Q)
                F += FILLS_Q + FILLS_K
                for i in range(FILLS_B):
                    plain_fill(F + i, i, b_hi[:, i % 2, i // 2, :])
                    done = place_queries(0, i)
                done.then_inc(qd_hi_ready, 1)
                F += FILLS_B
                for i in range(FILLS_V - 1):
                    plain_fill(F + i, i, v_hi[:, 2 * i:2 * i + 2, :].rearrange("p a c -> p (a c)"), CHUNK)
                    if i % 2 == 1:
                        done = place_queries(1, i // 2)
                done.then_inc(qd_hi_ready, 1)
                plain_fill(F + FILLS_V - 1, 0, v_hi[:, CHUNKS - 1, :], CHUNK, C)

            def exps(U, k):
                act.wait_ge(max_ready, U + 1)
                act.wait_ge(probT_ready, U + 1)
                act.wait_ge(rinv_done, U + 1)
                for j in range(2):
                    done = e.activation(prob[:, k % 2, j, 0:NKEY], ps_s[k % 2][:, j * NKEY:(j + 1) * NKEY],
                                        ACT.Exp, bias=negmax[:, k, j:j + 1], accum_out=rowsum[:, k, j:j + 1])
                done.then_inc(exp_done, 1)

            def probs_hi(U, k):
                act.wait_ge(probT_ready, U + 3)
                act.wait_ge(context_done, U + 1)
                e.activation(pt_hi[:, k % 2, :], ps_t[k % 2][0:CHUNK, :], ACT.Copy).then_inc(pt_hi_done, 1)

            def context_hi(I):
                act.wait_ge(ctxT_ready, I + 2)
                act.wait_ge(fc_done, I + 1)
                e.activation(ct_hi[:, :, :, :], ps_f[:, 0:256].rearrange("p (a h q) -> p a h q", a=2, h=2),
                             ACT.Copy).then_inc(ct_hi_done, 1)

            def turn(I, first, last):
                for k in range(4):
                    U = 4 * I + k
                    if k < 3 or not last:
                        exps(U + 1, (k + 1) % 4)
                    probs_hi(U, k)
                    if k == 1 and not first:
                        context_hi(I - 1)

            with act.Fori(0, B) as img:
                for i in range(FILLS_K):
                    k_fill(img * IMG_FILLS, i)
                def row(s, tail):
                    produce(img, s, tail)
                    I = (img * ROWS + s - 1) * TURNS
                    exps(4 * I, 0)
                    turn(I, True, False)
                    with act.Fori(1, TURNS - 1) as t:
                        turn(I + t, False, False)
                    turn(I + TURNS - 1, False, True)

                row(1, False)
                with act.Fori(2, ROWS + 1) as s:
                    row(s, True)
                context_hi((img + 1) * ROWS * TURNS - 1)

        @block.vector
        def _(dve):
            e = nc.vector
            for n, name in enumerate("qkvo"):
                dve.wait_ge(split_hi, n + 1)
                e.scalar_tensor_tensor(out=w_lo[name][:, :, :],
                                       in0=w32[:, 0:KC * C].rearrange("p (k c) -> p k c", k=KC), scalar=WS,
                                       in1=w_hi[name][:, :, :], op0=ALU.mult, op1=ALU.subtract)\
                    .then_inc(split_lo, 1)
            dve.wait_ge(split_hi, 5)
            e.scalar_tensor_tensor(out=rel_lo[:, :, :], in0=w32[:, :].rearrange("p (n c) -> p n c", n=NREL),
                                   scalar=WS, in1=rel_hi[:, :, :], op0=ALU.mult, op1=ALU.subtract)\
                .then_inc(split_lo, 1)
            dve.wait_ge(zeroed, NZERO)

            def stats_piece(r, t):
                n = KC * PIX // TURNS
                e.bn_stats(stats[:, bass.ds(r, 1), bass.ds(t, 1), :].rearrange("p a b n -> p (a b n)"),
                           st_load[:, bass.ds(t * n, n)]).then_inc(st_read, 1)

            with dve.Fori(0, ROWS) as r:
                dve.wait_ge(st_in, (r + 1) * 16)
                for t in range(TURNS):
                    stats_piece(r, t)

            def group_stats(img):
                dve.wait_ge(st_read, (img + 1) * ROWS * TURNS + 1)
                dve.sem_inc(dve_went_on, 1)
                for k in range(KC):
                    done = e.bn_aggr(agg[:, k, :], stats[:, :, 4 * k:4 * k + 4, :].rearrange("p r t n -> p r (t n)"))
                done.then_inc(gn_step, 1)
                dve.wait_ge(gn_mean, 2 * img + 1)
                e.tensor_copy(mean_sb[:, :], ps_p[0][:, 0:KC]).then_inc(gn_step, 1)
                dve.wait_ge(gn_step, 6 * img + 2)
                e.tensor_tensor(gn[:, 0, :], agg[:, :, 0], mean_sb[:, :], ALU.subtract).then_inc(gn_step, 1)
                dve.wait_ge(gn_step, 6 * img + 3)
                e.tensor_tensor(gn[:, 1, :], gn[:, 0, :], gn[:, 0, :], ALU.mult).then_inc(gn_step, 1)
                dve.wait_ge(gn_step, 6 * img + 4)
                e.tensor_tensor(gn[:, 2, :], gn[:, 1, :], agg[:, :, 1], ALU.add).then_inc(gn_step, 1)
                dve.wait_ge(gn_mean, 2 * img + 2)
                e.tensor_scalar(gn[:, 3, :], ps_p[0][:, KC:2 * KC], GN_EPS, None, ALU.add).then_inc(gn_step, 1)

            def k_fill(F, i):
                g, n = divmod(i, 2)
                dve.wait_ge(fill_hi, F + i + 1)
                for half in range(2):
                    r = slice(64 * half, 64 * half + 64)
                    at = (r, 2 * g + half, slice(HALO + 64 * n, HALO + 64 * n + 64), slice(WIN - BLK, WIN))
                    done = e.scalar_tensor_tensor(out=k_lo[at],
                                                  in0=ps_p[i % 2][r, :].rearrange("p (c r) -> p c r", r=BLK),
                                                  scalar=SCALE / WS, in1=k_hi[at],
                                                  op0=ALU.mult, op1=ALU.subtract)
                done.then_inc(fill_lo, 1)

            def plain_fill(F, i, to, high, rows=P, cols=512):
                dve.wait_ge(fill_hi, F + 1)
                e.scalar_tensor_tensor(out=to, in0=ps_p[i % 2][0:rows, 0:cols], scalar=1.0 / WS, in1=high,
                                       op0=ALU.mult, op1=ALU.subtract).then_inc(fill_lo, 1)

            def place(to, frm, m, hq, par, gs=slice(None)):
                r = slice(32 * m, 32 * m + 32)
                pairs = slice(hq // 2, None, 2) if gs == slice(None) else slice(2 * gs.start + hq // 2,
                                                                               2 * gs.start + hq // 2 + 1)
                return e.tensor_copy(to[r, pairs, par, :, hq % 2, :],
                                     frm[r, gs, par, :].rearrange("p g (t q) -> p g t q", q=NQ))

            def place_bias(i, par):
                m = i // 2
                return place(*((qd_hi, b_hi), (qd_lo, b_lo))[i % 2], m, (m + 2) % 4, par)

            def produce(img, s, tail):
                F = fills_before(img, s)
                last = (img * ROWS + s - 1) * TURNS - 1
                for i in range(FILLS_Q):
                    plain_fill(F + i, i, q_lo[:, i % 2, i // 2, :], q_hi[:, i % 2, i // 2, :])
                    if tail and i == 0:
                        normalise(last)
                    if tail and i == 1:
                        context_lo(last)
                    if tail and i == 2:
                        add_output(last, TURNS - 1)
                    if i == 0:
                        dve.wait_ge(fill_hi, F)
                        dve.wait_ge(fill_lo, F + 2)
                    r = slice(64 * (i // 2), 64 * (i // 2) + 64)
                    kk = (k_hi, k_lo)[i % 2]
                    done = e.tensor_copy(kk[r, i // 2::2, :, 0:WIN - BLK], kk[r, i // 2::2, :, BLK:WIN])
                done.then_inc(k_down, 1)
                dve.wait_ge(k_down, img * ROWS + s)
                for i in range(FILLS_K):
                    k_fill(F + FILLS_Q, i)
                dve.wait_ge(fill_lo, F + FILLS_Q + 2)
                F += FILLS_Q + FILLS_K
                for i in range(FILLS_B):
                    plain_fill(F + i, i, b_lo[:, i % 2, i // 2, :], b_hi[:, i % 2, i // 2, :])
                    if i < 2:
                        for hq in range(4):
                            done = place(qd_lo, q_lo, hq, hq, i)
                        done.then_inc(qd_lo_ready, 1)
                    else:
                        dve.wait_ge(fill_lo, F + 2 + 2)
                        for n in range(4):
                            done = place_bias(4 * (i - 2) + n, 0)
                done.then_inc(bd_ready, 1)
                F += FILLS_B
                dve.wait_ge(fill_lo, F + 2)
                for i in range(FILLS_V - 1):
                    plain_fill(F + i, i, v_lo[:, 2 * i:2 * i + 2, :].rearrange("p a c -> p (a c)"),
                               v_hi[:, 2 * i:2 * i + 2, :].rearrange("p a c -> p (a c)"), CHUNK)
                    done = place_bias(i, 1)
                done.then_inc(bd_ready, 1)
                plain_fill(F + FILLS_V - 1, 0, v_lo[:, CHUNKS - 1, :], v_hi[:, CHUNKS - 1, :], CHUNK, C)

            def maxima(U, k):
                dve.wait_ge(scores_ready, U + 1)
                e.tensor_reduce(negmax[:, k, :], ps_s[k % 2][:, 0:2 * NKEY].rearrange("p (j n) -> p j n", j=2),
                                AX.X, ALU.max, negate=True).then_inc(max_ready, 1)

            def probs_lo(U, k):
                dve.wait_ge(pt_hi_done, U + 1)
                e.tensor_tensor(pt_lo[:, k % 2, :], ps_t[k % 2][0:CHUNK, :], pt_hi[:, k % 2, :],
                                ALU.subtract).then_inc(pt_lo_done, 1)

            def reciprocals(U, k):
                dve.wait_ge(exp_done, U + 3)
                e.reciprocal(rinv[:, k, :], rowsum[:, k, :]).then_inc(rinv_done, 1)

            def normalise(I):
                dve.wait_ge(context_done, 4 * I + 4 + 2)
                dve.wait_ge(rinv_done, 4 * I + 4 + 4)
                dve.wait_ge(ctxT_ready, I + 1)
                for half in range(2):
                    r = slice(64 * half, 64 * half + 64)
                    done = e.tensor_tensor(ctxn[r, :, :, :].rearrange("p a b d -> p (a b) d"),
                                           ps_c[r, :].rearrange("p (u d) -> p u d", d=2 * DH)
                                           [:, :, DH * half:DH * half + DH],
                                           rinv[r, :, :].rearrange("p k j -> p (k j)").unsqueeze(2)
                                           .broadcast_to([64, 2 * PAIRS, DH]), ALU.mult)
                done.then_inc(norm_done, 1)

            def context_lo(I):
                dve.wait_ge(ct_hi_done, I + 1)
                e.tensor_tensor(ct_lo[:, :, :, :], ps_f[:, 0:256].rearrange("p (a h q) -> p a h q", a=2, h=2),
                                ct_hi[:, :, :, :], ALU.subtract).then_inc(ct_lo_done, 1)

            def add_output(I, t):
                dve.wait_ge(fc_done, I + 2)
                at = res[:, :, :, bass.ds(t * 2 * BLK, 2 * BLK)].rearrange("p k x c -> p (k x) c")
                e.scalar_tensor_tensor(out=at, in0=ps_f[:, 256:512].rearrange("p (m c) -> p m c", c=2 * BLK),
                                       scalar=1.0 / WS, in1=at, op0=ALU.mult, op1=ALU.add)\
                    .then_inc(out_added, 1)

            def turn(I, t, r, first, last):
                for k in range(4):
                    U = 4 * I + k
                    if k == 1 and not first:
                        normalise(I - 1)
                    if k == 2 and not first:
                        context_lo(I - 1)
                    if k == 3 and not first:
                        add_output(I - 1, t - 1)
                    if k < 2 or not last:
                        maxima(U + 2, (k + 2) % 4)
                    if k == 1:
                        dve.wait_ge(norm_done, I + 1)
                    if k > 0 or not first:
                        reciprocals(U - 1, (k - 1) % 4)
                    probs_lo(U, k)
                    if k == 2:
                        stats_piece(r, t)
                if last:
                    reciprocals(4 * I + 3, 3)

            with dve.Fori(0, B) as img:
                group_stats(img)
                for i in range(FILLS_K):
                    k_fill(img * IMG_FILLS, i)
                def row(s, tail):
                    produce(img, s, tail)
                    rr = img * ROWS + s - 1
                    I = rr * TURNS
                    dve.wait_ge(res_ready, rr + 1)
                    dve.wait_ge(st_in, (ROWS + rr + 1) * 16)
                    maxima(4 * I, 0)
                    maxima(4 * I + 1, 1)
                    turn(I, 0, s - 1, True, False)
                    with dve.Fori(1, TURNS - 1) as t:
                        turn(I + t, t, s - 1, False, False)
                    turn(I + TURNS - 1, TURNS - 1, s - 1, False, True)

                row(1, False)
                with dve.Fori(2, ROWS + 1) as s:
                    row(s, True)
                I = (img + 1) * ROWS * TURNS - 1
                normalise(I)
                context_lo(I)
                add_output(I, TURNS - 1)

        @block.tensor
        def _(pe):
            mm = nc.tensor.matmul
            pe.wait_ge(consts_in, 48)
            pe.wait_ge(zeroed, NZERO)
            pe.wait_ge(split_lo, 5)
            pe.wait_ge(onehot_in, 16 * PAIRS)

            def group_stats(img):
                pe.wait_ge(fill_lo, img * IMG_FILLS + 2)
                pe.wait_ge(gn_step, 6 * img + 1)
                mm(ps_p[0][:, 0:KC], gmean[:, :], agg[:, :, 0], start=True, stop=True).then_inc(gn_mean, 1)
                pe.wait_ge(gn_step, 6 * img + 5)
                mm(ps_p[0][:, KC:2 * KC], gmean[:, :], gn[:, 2, :], start=True, stop=True).then_inc(gn_mean, 1)

            def three(out_ap, terms, first=True, last=True):
                n = 3 * len(terms)
                i = 0
                for wh, wl, xh, xl in terms:
                    for a, b in ((wh, xh), (wh, xl), (wl, xh)):
                        done = mm(out_ap, a, b, start=first and i == 0, stop=last and i == n - 1,
                                  skip_group_check=True)
                        i += 1
                return done

            def bank_free(F, first):
                pe.wait_ge(fill_lo, F + (2 if first else 1))

            def k_fill(F, i):
                g, n = divmod(i, 2)
                bank_free(F + i, i == 0)
                cols = slice(HALO + 64 * n, HALO + 64 * n + 64)
                three(ps_p[i % 2][:, :],
                      [(w_hi["k"][:, k, g * P:(g + 1) * P], w_lo["k"][:, k, g * P:(g + 1) * P],
                        xn_hi[:, k, cols, WIN - BLK:WIN], xn_lo[:, k, cols, WIN - BLK:WIN])
                       for k in range(KC)]).then_inc(fill_done, 1)

            def q_fill(F, i):
                par, g = divmod(i, 2)
                bank_free(F + i, i == 0)

                def tokens(xn, k):
                    inside = xn[:, k, HALO:HALO + W, HALO:HALO + BLK]
                    return inside.rearrange("p (t a c) r -> p t a c r", a=2, c=BLK)[:, :, par, :, :]

                three(ps_p[i % 2][:, :],
                      [(w_hi["q"][:, k, g * P:(g + 1) * P], w_lo["q"][:, k, g * P:(g + 1) * P],
                        tokens(xn_hi, k), tokens(xn_lo, k)) for k in range(KC)]).then_inc(fill_done, 1)

            def v_fill(F, i, chunks):
                pe.wait_ge(fill_lo, F + 1)
                for j, c in enumerate(chunks):
                    for n, (k, a, b) in enumerate([(k, a, b) for k in range(KC)
                                                   for a, b in ((0, 0), (0, 1), (1, 0))]):
                        src = ((xn_hi, xn_lo)[a])[:, k, :, :].rearrange("p c r -> p (c r)")
                        done = mm(ps_p[i % 2][0:CHUNK, j * C:(j + 1) * C],
                                  src[:, bass.ds(c * CHUNK, CHUNK)],
                                  (w_hi, w_lo)[b]["v"][:, k, :], start=n == 0, stop=n == 5,
                                  skip_group_check=True)
                done.then_inc(fill_done, 1)

            def b_fill(F, i):
                par, g = divmod(i, 2)
                bank_free(F, False)
                acc = ps_p[i % 2][:, :].rearrange("p (t y x) -> p t y x", y=BLK, x=BLK)
                qh = q_hi[:, g, par, :].rearrange("p (t y x) -> p t y x", y=BLK, x=BLK)
                ql = q_lo[:, g, par, :].rearrange("p (t y x) -> p t y x", y=BLK, x=BLK)
                for y in range(BLK):
                    n = par * BLK + y
                    three(acc[:, :, y, :], [(rel_hi[:, n, :], rel_lo[:, n, :], qh[:, :, y, :], ql[:, :, y, :])],
                          first=y == 0, last=False)
                for xx in range(BLK):
                    n = 2 * BLK + xx
                    done = three(acc[:, :, :, xx], [(rel_hi[:, n, :], rel_lo[:, n, :],
                                                     qh[:, :, :, xx], ql[:, :, :, xx])],
                                 first=False, last=xx == BLK - 1)
                done.then_inc(fill_done, 1)

            def produce(img, s, tail):
                F = fills_before(img, s)
                I = (img * ROWS + s - 1) * TURNS
                pe.wait_ge(xn_ready, img * (ROWS + 1) + s + 1)
                for i in range(FILLS_Q):
                    q_fill(F, i)
                    if tail and i == 0:
                        context(4 * I - 1, 3, TURNS - 1, I - 1)
                    if tail and i == 1:
                        transpose_context(I - 1)
                    if tail and i == 2:
                        output(I - 1)
                for i in range(FILLS_K):
                    k_fill(F + FILLS_Q, i)
                F += FILLS_Q + FILLS_K
                pe.wait_ge(fill_lo, F - FILLS_K + 2)
                for i in range(FILLS_B):
                    b_fill(F + i, i)
                F += FILLS_B
                with pe.Fori(0, 4) as v:
                    for i in range(2):
                        v_fill(F + 2 * v + i, i, (4 * v + 2 * i, 4 * v + 2 * i + 1))
                pe.wait_ge(qd_hi_ready, 2 * (img * ROWS + s) - 1)
                pe.wait_ge(qd_lo_ready, 2 * (img * ROWS + s) - 1)
                pe.wait_ge(bd_ready, 2 * (img * ROWS + s) - 1)
                scores(4 * I, 0, 0)
                scores(4 * I + 1, 1, 0)
                v_fill(F + FILLS_V - 1, 0, (CHUNKS - 1,))

            def scores(U, k, t):
                par, g = divmod(k, 2)
                pe.wait_ge(exp_done, U + 1)
                for j in range(2):
                    p = 2 * g + j

                    def queries(qd):
                        return qd[:, p, par, :, :, :].rearrange("p t h q -> p (t h q)")[
                            :, bass.ds(t * 2 * NQ, 2 * NQ)]

                    def keys(kk):
                        return kk[:, p, :, :].rearrange("p c r -> p (c r)")[
                            :, bass.ds((2 * t + par) * CHUNK, NKEY)]

                    done = three(ps_s[k % 2][:, j * NKEY:(j + 1) * NKEY],
                                 [(queries(qd_hi), queries(qd_lo), keys(k_hi), keys(k_lo))])
                done.then_inc(scores_ready, 1)

            def transpose_probs(U, k):
                pe.wait_ge(exp_done, U + 3)
                pe.wait_ge(pt_lo_done, U + 1)
                for j in range(2):
                    for c in range(2):
                        at = (2 * j + c) * P
                        done = nc.tensor.transpose(ps_t[k % 2][0:CHUNK, at:at + P],
                                                   prob[:, k % 2, j, c * CHUNK:(c + 1) * CHUNK], ident[:, :])
                done.then_inc(probT_ready, 1)

            def context(U, k, t, I):
                par, g = divmod(k, 2)
                pe.wait_ge(pt_lo_done, U + 3)
                if k == 0:
                    pe.wait_ge(norm_done, I + 1)
                for j in range(2):
                    p = 2 * g + j
                    terms = []
                    for c in range(2):
                        at = (2 * j + c) * P

                        def values(v):
                            return v[:, bass.ds(2 * t + par + c, 1), p * 2 * DH:(p + 1) * 2 * DH]\
                                .rearrange("p a c -> p (a c)")

                        terms.append((pt_hi[:, k % 2, at:at + P], pt_lo[:, k % 2, at:at + P],
                                      values(v_hi), values(v_lo)))
                    at = (par * PAIRS + p) * 2 * DH
                    done = three(ps_c[:, at:at + 2 * DH], terms)
                done.then_inc(context_done, 1)

            def transpose_context(I):
                pe.wait_ge(norm_done, I + 2)
                pe.wait_ge(out_added, I + 1)
                for par in range(2):
                    done = nc.tensor.transpose(ps_f[:, par * P:(par + 1) * P],
                                               ctxn[:, par, :, :].rearrange("p a d -> p (a d)"), ident[:, :])
                done.then_inc(ctxT_ready, 1)

            def output(I):
                pe.wait_ge(ct_lo_done, I + 1)

                def tokens(ct, half):
                    return ct[:, :, half, :].rearrange("p a (y x) -> p x a y", y=BLK)

                for k in range(KC):
                    done = three(ps_f[:, 256 + k * P:256 + (k + 1) * P],
                                 [(w_hi["o"][:, half, k * P:(k + 1) * P], w_lo["o"][:, half, k * P:(k + 1) * P],
                                   tokens(ct_hi, half), tokens(ct_lo, half)) for half in range(2)])
                done.then_inc(fc_done, 1)

            def turn(I, t, first, last):
                for k in range(4):
                    U = 4 * I + k
                    transpose_probs(U, k)
                    if k < 2:
                        scores(U + 2, k + 2, t)
                    elif not last:
                        scores(U + 2, k - 2, t + 1)
                    if k == 1 and not first:
                        transpose_context(I - 1)
                    if k > 0:
                        context(U - 1, k - 1, t, I)
                    elif not first:
                        context(U - 1, 3, t - 1, I - 1)
                    if k == 2 and not first:
                        output(I - 1)

            with pe.Fori(0, B) as img:
                group_stats(img)
                pe.wait_ge(xn_ready, img * (ROWS + 1) + 1)
                for i in range(FILLS_K):
                    k_fill(img * IMG_FILLS, i)
                def row(s, tail):
                    produce(img, s, tail)
                    rr = img * ROWS + s - 1
                    I = rr * TURNS
                    pe.wait_ge(qd_hi_ready, 2 * rr + 2)
                    pe.wait_ge(qd_lo_ready, 2 * rr + 2)
                    pe.wait_ge(bd_ready, 2 * rr + 2)
                    turn(I, 0, True, False)
                    with pe.Fori(1, TURNS - 1) as t:
                        turn(I + t, t, False, False)
                    turn(I + TURNS - 1, TURNS - 1, False, True)

                row(1, False)
                with pe.Fori(2, ROWS + 1) as s:
                    row(s, True)
                I = (img + 1) * ROWS * TURNS
                context(4 * I - 1, 3, TURNS - 1, I - 1)
                transpose_context(I - 1)
                output(I - 1)


def _relative_weights(np, rel_w, rel_h):
    full = np.zeros((P, NREL, P), np.float32)
    for m in range(4):
        hq = (m + 2) % 4
        rows = slice(DH * hq, DH * hq + DH)
        for n in range(NREL):
            q = n % BLK
            for j in range(WIN):
                if n < 2 * BLK:
                    full[rows, n, 32 * m + (j + BLK * (n // BLK)) % 16] = rel_w[j - q + WIN - 1]
                else:
                    full[rows, n, 32 * m + 16 + j] = rel_h[j - q + WIN - 1]
    return full.reshape(P, NREL * P)


def kernel(**inputs):
    import numpy as _np
    import concourse.bacc as _bacc
    from concourse import mybir as _mybir
    from concourse.bass_utils import run_bass_kernel_spmd as _run

    a = {n: _np.asarray(v) for n, v in inputs.items()}
    x, w_q, w_kv = a["x"], a["L0_conv_w_q"], a["L0_conv_w_kv"]
    fc_w, fc_b = a["L0_conv_fc_w"], a["L0_conv_fc_b"]

    def halves(w):
        return w.T.reshape(KC, P, C).transpose(1, 0, 2).reshape(P, KC * C)

    fc = fc_w.T.reshape(PAIRS, 2, DH, C).transpose(1, 0, 2, 3).reshape(KC, P, C)
    col, row = _np.arange(WP)[:, None], _np.arange(WIN)[None, :]
    onehot = _np.zeros((P, WP, WIN), _np.float16)
    for m in range(4):
        for r in range(16):
            onehot[32 * m + r] = (col % 16 == r) & (row >= 0)
        for i in range(WIN):
            onehot[32 * m + 16 + i] = (row == i) & (col >= 0)
    gmean = _np.kron(_np.eye(P // CG), _np.full((CG, CG), 1.0 / CG)).astype(_np.float32)
    arrays = {
        "x": x, "wqT": halves(w_q), "wkT": halves(w_kv[:C]), "wvT": halves(w_kv[C:]),
        "fcT": fc.transpose(1, 0, 2).reshape(P, KC * C), "fcb": fc_b.reshape(KC, P).T,
        "rel": _relative_weights(_np, a["L0_conv_rel_w"], a["L0_conv_rel_h"]), "onehot": onehot,
        "ident": _np.eye(P, dtype=_np.float32), "gmean": gmean,
    }
    arrays = {n: _np.ascontiguousarray(v) for n, v in arrays.items()}
    nc = _bacc.Bacc("TRN2", target_bir_lowering=False, num_devices=1)
    args = [nc.dram_tensor(f"in_{n}", v.shape, _mybir.dt.from_np(v.dtype), kind="ExternalInput").ap()
            for n, v in arrays.items()]
    args.append(nc.dram_tensor("out_0", x.shape, _mybir.dt.float32, kind="ExternalOutput").ap())
    halo_attention_program(nc, *args)
    r = _run(nc, [{f"in_{n}": v for n, v in arrays.items()}], core_ids=[0])
    return r.results[0]["out_0"]
```

```python
from contextlib import ExitStack

import concourse.bass as bass
from concourse import mybir

F32 = mybir.dt.float32
F16 = mybir.dt.float16
U32 = mybir.dt.uint32
ALU = mybir.AluOpType
ACT = mybir.ActivationFunctionType
AX = mybir.AxisListType

P = 128
C, H, W = 256, 128, 128
HEADS, DH = 8, 32
BLK, HALO = 8, 3
WIN = BLK + 2 * HALO
NKEY = WIN * WIN
NQ = BLK * BLK
GROUPS, GN_EPS = 32, 1e-5
CG = C // GROUPS
KC = C // P
ROWS = H // BLK
TURNS = W // BLK // 2
WP = W + BLK
CHUNK = BLK * WIN
CHUNKS = WP // BLK
PADK = 2 * CHUNK
PAIRS = HEADS // 2
PIX = BLK * W
NREL = 3 * BLK
WS = 64.0
SCALE = float(DH) ** -0.5
ORDER = [("q", 0), ("q", 1), ("q", 2), ("q", 3), ("b", 0), ("b", 1), ("v", 0), ("k", 0), ("v", 1), ("k", 1),
         ("b", 2), ("b", 3), ("v", 2), ("k", 2), ("v", 3), ("k", 3), ("v", 4), ("v", 5), ("v", 6), ("v", 7),
         ("v", 8)]
FILLS_K = 4
FILLS = len(ORDER)
NWORD = 6


def halo_attention_program(nc, x, wqT, wkT, wvT, fcT, fcb, rel, onehot, ident_in, gmean_in, out):
    B = x.shape[0]
    IMG_FILLS = FILLS_K + ROWS * FILLS

    with ExitStack() as ctx:
        def sb(name, shape, dt):
            return ctx.enter_context(nc.sbuf_tensor(name, shape, dt))

        def psum(name):
            return ctx.enter_context(nc.psum_tensor(name, [P, 512], F32))

        def sem(name):
            return ctx.enter_context(nc.semaphore(name))

        ident = sb("ident", [P, P], F32)
        gmean = sb("gmean", [P, P], F32)
        w32 = sb("w32", [P, NREL * P], F32)
        w_hi = {n: sb(f"w{n}_hi", [P, KC, C], F16) for n in "qkvo"}
        w_lo = {n: sb(f"w{n}_lo", [P, KC, C], F16) for n in "qkvo"}
        rel_hi = sb("rel_hi", [P, NREL, P], F16)
        rel_lo = sb("rel_lo", [P, NREL, P], F16)
        fcb_sb = sb("fcb_sb", [P, KC], F32)
        x_load = sb("x_load", [P, KC, BLK, W], F32)
        x_top = sb("x_top", [P, KC, HALO, W], F32)
        x_norm = sb("x_norm", [P, KC, BLK, W], F32)
        st_load = sb("st_load", [P, KC * PIX], F32)
        stats = sb("stats", [P, ROWS, TURNS, NWORD], F32)
        gn = sb("gn", [P, 8, KC], F32)
        agg = sb("agg", [P, KC, 2], F32)
        mean_sb = sb("mean_sb", [P, KC], F32)
        rstd_sb = sb("rstd_sb", [P, KC], F32)
        xn_hi = sb("xn_hi", [P, KC, WP, WIN], F16)
        xn_lo = sb("xn_lo", [P, KC, WP, WIN], F16)
        k_hi = sb("k_hi", [P, PAIRS, WP, WIN], F16)
        k_lo = sb("k_lo", [P, PAIRS, WP, WIN], F16)
        q_hi = sb("q_hi", [P, 2, 2, TURNS * NQ], F16)
        q_lo = sb("q_lo", [P, 2, 2, TURNS * NQ], F16)
        b_hi = sb("b_hi", [P, 2, 2, TURNS * NQ], F16)
        b_lo = sb("b_lo", [P, 2, 2, TURNS * NQ], F16)
        qd_hi = sb("qd_hi", [P, PAIRS, 2, TURNS, 2, NQ], F16)
        qd_lo = sb("qd_lo", [P, PAIRS, 2, TURNS, 2, NQ], F16)
        v_hi = sb("v_hi", [CHUNK, CHUNKS, C], F16)
        v_lo = sb("v_lo", [CHUNK, CHUNKS, C], F16)
        negmax = sb("negmax", [P, 4, 2], F32)
        rowsum = sb("rowsum", [P, 2, 4, 2], F32)
        rinv = sb("rinv", [P, 4, 2], F32)
        prob = sb("prob", [P, 2, 2, PADK], F32)
        pt_hi = sb("pt_hi", [CHUNK, 2, 512], F16)
        pt_lo = sb("pt_lo", [CHUNK, 2, 512], F16)
        ctxn = sb("ctxn", [P, 2, PAIRS, DH], F32)
        ct_hi = sb("ct_hi", [P, 2, 2, NQ], F16)
        ct_lo = sb("ct_lo", [P, 2, 2, NQ], F16)
        res = sb("res", [P, KC, BLK, W], F32)

        ps_s = [psum(f"ps_scores{i}") for i in range(2)]
        ps_t = [psum(f"ps_probT{i}") for i in range(2)]
        ps_c = [psum(f"ps_context{i}") for i in range(2)]
        ps_f = psum("ps_output")
        ps_p = [psum("ps_project"), ps_t[0], ps_t[1], ps_c[1]]

        weights_in = sem("weights_in")
        consts_in = sem("consts_in")
        split_hi = sem("split_hi")
        split_lo = sem("split_lo")
        zeroed = sem("zeroed")
        onehot_in = sem("onehot_in")
        st_in = sem("st_in")
        st2_in = sem("st2_in")
        st_read = sem("st_read")
        gn_step = sem("gn_step")
        gn_mean = sem("gn_mean")
        gn_ready = sem("gn_ready")
        x_in = sem("x_in")
        top_in = sem("top_in")
        top_scaled = sem("top_scaled")
        top_hi = sem("top_hi")
        x_read = sem("x_read")
        pool_step = sem("pool_step")
        xn_ready = sem("xn_ready")
        res_in = sem("res_in")
        res_ready = sem("res_ready")
        out_stored = sem("out_stored")
        pool_went_on = sem("pool_went_on")
        dve_went_on = sem("dve_went_on")
        sp_went_on = sem("sp_went_on")
        fill_done = sem("fill_done")
        fill_hi = sem("fill_hi")
        fill_lo = sem("fill_lo")
        k_down = sem("k_down")
        qd_hi_ready = sem("qd_hi_ready")
        qd_lo_ready = sem("qd_lo_ready")
        bd_ready = sem("bd_ready")
        scores_ready = sem("scores_ready")
        max_ready = sem("max_ready")
        exp_done = sem("exp_done")
        probT_ready = sem("probT_ready")
        pt_hi_done = sem("pt_hi_done")
        pt_lo_done = sem("pt_lo_done")
        context_done = sem("context_done")
        rinv_done = sem("rinv_done")
        norm_done = sem("norm_done")
        ctxT_ready = sem("ctxT_ready")
        ct_hi_done = sem("ct_hi_done")
        ct_lo_done = sem("ct_lo_done")
        fc_done = sem("fc_done")
        out_added = sem("out_added")

        CREDITS = [(exp_done, 2), (probT_ready, 2), (pt_lo_done, 2), (context_done, 2),
                   (norm_done, 2), (ctxT_ready, 1), (fc_done, 1), (out_added, 1), (fill_done, 1),
                   (fill_lo, 2), (st_read, TURNS + 1), (x_read, 1), (out_stored, 16)]
        NZERO = 8
        scratch = sb("scratch", [P, len(CREDITS)], F32)
        mhalf = sb("mhalf", [P, KC], F32)

        block = ctx.enter_context(nc.Block())

        def fills_before(img, s):
            return img * IMG_FILLS + FILLS_K + (s - 1) * FILLS

        @block.sync
        def _(sp):
            sp.dma_start(ident[:, :], ident_in).then_inc(consts_in, 16)
            sp.dma_start(gmean[:, :], gmean_in).then_inc(consts_in, 16)
            sp.dma_start(fcb_sb[:, :], fcb).then_inc(consts_in, 16)
            x_pix = x.rearrange("b (k p) h w -> p b k (h w)", p=P)
            out_pix = out.rearrange("b (k p) h w -> p b k (h w)", p=P)

            def load_stats(img, r, to, signal):
                sp.dma_start(to.rearrange("p (k n) -> p k n", k=KC),
                             x_pix[:, bass.ds(img, 1), :, bass.ds(r * PIX, PIX)]
                             .rearrange("p a k n -> p (a k) n")).then_inc(signal, 16)

            res_flat = res[:, :, :, :].rearrange("p k r w -> p (k r w)")

            def load_top(img):
                for k in range(KC):
                    sp.dma_start(x_top[:, k, :, :].rearrange("p r w -> p (r w)"),
                                 x_pix[:, bass.ds(img, 1), k, 0:HALO * W]
                                 .rearrange("p a n -> p (a n)")).then_inc(top_in, 16)

            def load_strip(img, n, first_row, rows):
                sp.wait_ge(x_read, n + 1)
                for k in range(KC):
                    sp.dma_start(x_load[:, k, 0:rows, :].rearrange("p r w -> p (r w)"),
                                 x_pix[:, bass.ds(img, 1), k, bass.ds(first_row * W, rows * W)]
                                 .rearrange("p a n -> p (a n)")).then_inc(x_in, 16)

            def load_residual(img, s):
                sp.wait_ge(out_stored, ((img * ROWS + s - 1) * KC + 1) * 16)
                for k in range(KC):
                    sp.dma_start(res[:, k, :, :].rearrange("p r w -> p (r w)"),
                                 x_pix[:, bass.ds(img, 1), k, bass.ds((s - 1) * PIX, PIX)]
                                 .rearrange("p a n -> p (a n)")).then_inc(res_in, 16)

            def store_row(img, s):
                sp.wait_ge(out_added, (img * ROWS + s) * TURNS + 1)
                for k in range(KC):
                    sp.dma_start(out_pix[:, bass.ds(img, 1), k, bass.ds((s - 1) * PIX, PIX)]
                                 .rearrange("p a n -> p (a n)"),
                                 res[:, k, :, :].rearrange("p r w -> p (r w)")).then_inc(out_stored, 16)

            with sp.Fori(0, ROWS // 2) as r:
                for i, (to, signal) in enumerate(((st_load[:, :], st_in), (res_flat, st2_in))):
                    sp.wait_ge(st_read, (2 * r + i) * TURNS + 1)
                    load_stats(0, 2 * r + i, to, signal)
            load_top(0)
            load_strip(0, 0, HALO, BLK)
            with sp.Fori(0, B) as img:

                def row(s):
                    rr = img * ROWS + s - 1
                    sp.wait_ge(st_read, (ROWS + rr + 1) * TURNS + 1)
                    load_stats((img + 1) % B, s - 1, st_load[:, :], st_in)
                    load_residual(img, s)

                with sp.Fori(1, ROWS - 1) as s:
                    row(s)
                    load_strip(img, img * ROWS + s, s * BLK + HALO, BLK)
                    store_row(img, s)
                row(ROWS - 1)
                load_strip(img, img * ROWS + ROWS - 1, (ROWS - 1) * BLK + HALO, BLK - HALO)
                sp.wait_ge(xn_ready, img * ROWS + 1)
                sp.sem_inc(sp_went_on, 1)
                load_top((img + 1) % B)
                store_row(img, ROWS - 1)
                row(ROWS)
                load_strip((img + 1) % B, (img + 1) * ROWS, HALO, BLK)
                store_row(img, ROWS)
            sp.wait_ge(out_stored, (B * ROWS * KC + 1) * 16)

        @block.gpsimd
        def _(pool):
            g = nc.gpsimd
            for at, (s, n) in enumerate(CREDITS):
                g.memset(scratch[:, at:at + 1], 0.0).then_inc(s, n)
            g.memset(k_hi[:, :, :, :], 0.0).then_inc(zeroed, 1)
            g.memset(k_lo[:, :, :, :], 0.0).then_inc(zeroed, 1)
            g.memset(xn_hi[:, :, :, :], 0.0).then_inc(zeroed, 1)
            g.memset(xn_lo[:, :, :, :], 0.0).then_inc(zeroed, 1)
            g.memset(qd_hi[:, :, :, :, :, :], 0.0).then_inc(zeroed, 1)
            g.memset(qd_lo[:, :, :, :, :, :], 0.0).then_inc(zeroed, 1)
            g.memset(prob[:, :, :, :], 0.0).then_inc(zeroed, 1)
            g.memset(mhalf[:, :], -0.5).then_inc(zeroed, 1)
            pool.wait_ge(zeroed, NZERO)
            pool.wait_ge(consts_in, 48)

            inner = slice(HALO, HALO + W)
            keep = WIN - BLK

            def prepare_strip(img, s, last):
                n = img * ROWS + s - 1
                step = 3 * (img * (ROWS - 1) + s - 2)
                pool.wait_ge(fill_done, fills_before(img, s - 1) + FILLS + 1)
                pool.sem_inc(pool_went_on, 1)
                g.tensor_scalar(xn_hi[:, :, :, 0:keep], xn_hi[:, :, :, BLK:WIN], 1.0, None, ALU.mult)
                copied = g.tensor_scalar(xn_lo[:, :, :, 0:keep], xn_lo[:, :, :, BLK:WIN], 1.0, None, ALU.mult)
                at, rows = keep, BLK
                if last:
                    copied.then_inc(pool_step, 1)
                    pool.wait_ge(pool_step, step + 1)
                    pool.sem_inc(pool_went_on, 1)
                    rows = BLK - HALO
                    g.memset(xn_hi[:, :, :, WIN - HALO:WIN], 0.0)
                    g.memset(xn_lo[:, :, :, WIN - HALO:WIN], 0.0).then_inc(pool_step, 1)
                else:
                    copied.then_inc(pool_step, 2)
                pool.wait_ge(x_in, (n + 1) * KC * 16)
                pool.sem_inc(pool_went_on, 1)
                for k in range(KC):
                    done = g.tensor_scalar(x_norm[:, k, 0:rows, :], x_load[:, k, 0:rows, :],
                                           mean_sb[:, k:k + 1], rstd_sb[:, k:k + 1],
                                           ALU.subtract, ALU.mult)
                done.then_inc(x_read, 1)
                pool.wait_ge(x_read, n + 2)
                pool.wait_ge(pool_step, step + 2)
                pool.sem_inc(pool_went_on, 1)
                columns = x_norm[:, :, 0:rows, :].rearrange("p k r w -> p k w r")
                for k in range(KC):
                    done = g.tensor_scalar(xn_hi[:, k, inner, at:at + rows], columns[:, k, :, :], 1.0, None,
                                           ALU.mult)
                done.then_inc(pool_step, 1)
                pool.wait_ge(pool_step, step + 3)
                pool.sem_inc(pool_went_on, 1)
                for k in range(KC):
                    done = g.tensor_tensor(xn_lo[:, k, inner, at:at + rows], columns[:, k, :, :],
                                           xn_hi[:, k, inner, at:at + rows], ALU.subtract)
                done.then_inc(xn_ready, 1)

            def place_queries(img, s):
                pool.wait_ge(xn_ready, img * ROWS + s)
                pool.sem_inc(pool_went_on, 1)
                for par in range(2):
                    pool.wait_ge(fill_lo, fills_before(img, s) + 2 * par + 2 + 2)
                    pool.sem_inc(pool_went_on, 1)
                    for hq in range(4):
                        r = slice(32 * hq, 32 * hq + 32)
                        done = g.tensor_copy(qd_lo[r, hq // 2::2, par, :, hq % 2, :].bitcast(U32),
                                             q_lo[r, :, par, :].rearrange("p g (t q) -> p g t q", q=NQ)
                                             .bitcast(U32))
                    done.then_inc(qd_lo_ready, 1)

            def row(img, s):
                place_queries(img, s)
                rr = img * ROWS + s - 1
                pool.wait_ge(qd_lo_ready, 2 * rr + 2)
                pool.sem_inc(pool_went_on, 1)
                pool.wait_ge(res_in, (rr + 1) * KC * 16)
                pool.sem_inc(pool_went_on, 1)
                for k in range(KC):
                    done = g.tensor_scalar(res[:, k, :, :], res[:, k, :, :], fcb_sb[:, k:k + 1], None, ALU.add)
                done.then_inc(res_ready, 1)

            with pool.Fori(0, B) as img:
                pool.wait_ge(gn_step, 6 * img + 6)
                pool.sem_inc(pool_went_on, 1)
                g.tensor_tensor(rstd_sb[:, :], gn[:, 3, :], mhalf[:, :], ALU.pow).then_inc(gn_ready, 1)
                with pool.Fori(1, ROWS - 1) as s:
                    row(img, s)
                    prepare_strip(img, s + 1, False)
                row(img, ROWS - 1)
                prepare_strip(img, ROWS, True)
                row(img, ROWS)

        @block.scalar
        def _(act):
            e = nc.scalar
            for n, w in enumerate((wqT, wkT, wvT, fcT)):
                act.dma_start(w32[:, n * KC * C:(n + 1) * KC * C], w).then_inc(weights_in, 16)
            for n, name in enumerate("qkvo"):
                act.wait_ge(weights_in, 16 * 4)
                e.activation(w_hi[name][:, :, :],
                             w32[:, n * KC * C:(n + 1) * KC * C].rearrange("p (k c) -> p k c", k=KC),
                             ACT.Copy, scale=WS).then_inc(split_hi, 1)
            act.wait_ge(split_lo, 4)
            act.dma_start(w32[:, :], rel).then_inc(weights_in, 16)
            act.wait_ge(weights_in, 16 * 5)
            e.activation(rel_hi[:, :, :], w32[:, :].rearrange("p (n c) -> p n c", n=NREL),
                         ACT.Copy, scale=WS).then_inc(split_hi, 1)
            act.wait_ge(zeroed, NZERO)
            for p in range(PAIRS):
                r0 = 64 if p % 2 == 0 else 0
                act.dma_start(k_hi[r0:r0 + 64, p, :, :], onehot[r0:r0 + 64, :, :]).then_inc(onehot_in, 16)

            def top_strip(img):
                for k in range(KC):
                    act.wait_ge(top_scaled, KC * img + k + 1)
                    e.activation(xn_hi[:, k, HALO:HALO + W, HALO:2 * HALO],
                                 x_top[:, k, :, :].rearrange("p r w -> p w r"), ACT.Copy)
                    e.activation(xn_hi[:, k, HALO:HALO + W, 2 * HALO:WIN],
                                 x_norm[:, k, :, :].rearrange("p r w -> p w r"), ACT.Copy).then_inc(top_hi, 1)

            def k_fill(F, j, i, rows=slice(WIN - BLK, WIN)):
                g, n = divmod(i, 2)
                act.wait_ge(fill_done, F + j + 2)
                for half in range(2):
                    r = slice(64 * half, 64 * half + 64)
                    done = e.activation(k_hi[r, 2 * g + half, HALO + 64 * n:HALO + 64 * n + 64, rows],
                                        ps_p[j % 4][r, 0:64 * (rows.stop - rows.start)]
                                        .rearrange("p (c r) -> p c r", c=64),
                                        ACT.Copy, scale=SCALE / WS)
                done.then_inc(fill_hi, 1)

            def plain_fill(F, j, to, rows=P, cols=512):
                act.wait_ge(fill_done, F + j + 2)
                e.activation(to, ps_p[j % 4][0:rows, 0:cols], ACT.Copy, scale=1.0 / WS).then_inc(fill_hi, 1)

            def place_queries(par, hq):
                r = slice(32 * hq, 32 * hq + 32)
                return e.activation(qd_hi[r, hq // 2::2, par, :, hq % 2, :],
                                    q_hi[r, :, par, :].rearrange("p g (t q) -> p g t q", q=NQ), ACT.Copy)

            def produce(img, s, tail):
                F = fills_before(img, s)
                for j, (kind, i) in enumerate(ORDER):
                    if kind == "q":
                        plain_fill(F, j, q_hi[:, i % 2, i // 2, :])
                        if tail and i == 1:
                            context_hi((img * ROWS + s - 1) * TURNS - 1)
                    elif kind == "b":
                        if i == 0:
                            act.wait_ge(fill_hi, F + 4)
                        plain_fill(F, j, b_hi[:, i % 2, i // 2, :])
                        place_queries(i // 2, i % 2)
                    elif kind == "k":
                        if tail and i == 0:
                            act.wait_ge(k_down, img * (ROWS - 1) + s - 1)
                        k_fill(F, j, i)
                    elif i < 8:
                        plain_fill(F, j, v_hi[:, 2 * i:2 * i + 2, :].rearrange("p a c -> p (a c)"), CHUNK)
                        if i == 6:
                            exps((img * ROWS + s - 1) * TURNS, 0, 0)
                        if i < 4:
                            done = place_queries(i // 2, 2 + i % 2)
                            if i % 2 == 1:
                                done.then_inc(qd_hi_ready, 1)
                    else:
                        plain_fill(F, j, v_hi[:, CHUNKS - 1, :], CHUNK, C)

            def exps(I, k, buf):
                U = 4 * I + k
                act.wait_ge(max_ready, U + 1)
                for j in range(2):
                    done = e.activation(prob[:, k % 2, j, 0:NKEY], ps_s[k % 2][:, j * NKEY:(j + 1) * NKEY],
                                        ACT.Exp, bias=negmax[:, k, j:j + 1], accum_out=rowsum[:, buf, k, j:j + 1])
                done.then_inc(exp_done, 1)

            def probs_hi(U, k):
                act.wait_ge(probT_ready, U + 3)
                act.wait_ge(context_done, U + 1)
                e.activation(pt_hi[:, k % 2, :], ps_t[k % 2][0:CHUNK, :], ACT.Copy).then_inc(pt_hi_done, 1)

            def context_hi(I):
                act.wait_ge(ctxT_ready, I + 2)
                act.wait_ge(fc_done, I + 1)
                e.activation(ct_hi[:, :, :, :], ps_f[:, 0:256].rearrange("p (a h q) -> p a h q", a=2, h=2),
                             ACT.Copy).then_inc(ct_hi_done, 1)

            def turn(I, buf, first, last):
                for k in range(4):
                    if k < 3:
                        exps(I, k + 1, buf)
                    elif not last:
                        exps(I + 1, 0, 1 - buf)
                    probs_hi(4 * I + k, k)
                    if k == 1 and not first:
                        context_hi(I - 1)

            with act.Fori(0, B) as img:
                top_strip(img)
                for i in range(FILLS_K):
                    k_fill(img * IMG_FILLS, i, i, slice(0, WIN - BLK))

                def row(s, tail):
                    produce(img, s, tail)
                    I = (img * ROWS + s - 1) * TURNS
                    turn(I, 0, True, False)
                    with act.Fori(0, TURNS // 2 - 1) as t:
                        turn(I + 2 * t + 1, 1, False, False)
                        turn(I + 2 * t + 2, 0, False, False)
                    turn(I + TURNS - 1, 1, False, True)

                row(1, False)
                with act.Fori(2, ROWS + 1) as s:
                    row(s, True)
                context_hi((img + 1) * ROWS * TURNS - 1)

        @block.vector
        def _(dve):
            e = nc.vector
            for n, name in enumerate("qkvo"):
                dve.wait_ge(split_hi, n + 1)
                e.scalar_tensor_tensor(out=w_lo[name][:, :, :],
                                       in0=w32[:, n * KC * C:(n + 1) * KC * C].rearrange("p (k c) -> p k c", k=KC),
                                       scalar=WS, in1=w_hi[name][:, :, :], op0=ALU.mult, op1=ALU.subtract)\
                    .then_inc(split_lo, 1)

            def stats_piece(r, t, frm):
                n = KC * PIX // TURNS
                e.bn_stats(stats[:, bass.ds(r, 1), bass.ds(t, 1), :].rearrange("p a b n -> p (a b n)"),
                           frm[:, bass.ds(t * n, n)]).then_inc(st_read, 1)

            with dve.Fori(0, ROWS // 2) as r:
                for i, (frm, signal) in enumerate(((st_load, st_in),
                                                   (res[:, :, :, :].rearrange("p k r w -> p (k r w)"), st2_in))):
                    dve.wait_ge(signal, (r + 1) * 16)
                    for t in range(TURNS):
                        stats_piece(2 * r + i, t, frm)
            dve.wait_ge(split_hi, 5)
            e.scalar_tensor_tensor(out=rel_lo[:, :, :], in0=w32[:, :].rearrange("p (n c) -> p n c", n=NREL),
                                   scalar=WS, in1=rel_hi[:, :, :], op0=ALU.mult, op1=ALU.subtract)\
                .then_inc(split_lo, 1)
            dve.wait_ge(zeroed, NZERO)

            def top_strip(img):
                dve.wait_ge(fill_done, img * IMG_FILLS + 1)
                for xn in (xn_hi, xn_lo):
                    e.memset(xn[:, :, :, 0:HALO], 0.0)
                dve.wait_ge(top_in, (img + 1) * KC * 16)
                dve.wait_ge(x_in, (img * ROWS + 1) * KC * 16)
                dve.wait_ge(gn_ready, img + 1)
                for k in range(KC):
                    for to, frm in ((x_top, x_top), (x_norm, x_load)):
                        done = e.tensor_scalar(to[:, k, :, :], frm[:, k, :, :], mean_sb[:, k:k + 1],
                                               rstd_sb[:, k:k + 1], ALU.subtract, ALU.mult)
                    done.then_inc(top_scaled, 1)
                dve.wait_ge(top_scaled, KC * img + KC)
                dve.sem_inc(x_read, 1)
                for k in range(KC):
                    dve.wait_ge(top_hi, KC * img + k + 1)
                    for frm, at in ((x_top, slice(HALO, 2 * HALO)), (x_norm, slice(2 * HALO, WIN))):
                        done = e.tensor_tensor(xn_lo[:, k, HALO:HALO + W, at],
                                               frm[:, k, :, :].rearrange("p r w -> p w r"),
                                               xn_hi[:, k, HALO:HALO + W, at], ALU.subtract)
                done.then_inc(xn_ready, 1)

            def group_stats(img):
                dve.wait_ge(st_read, ((img + 1) * ROWS + 1) * TURNS + 1)
                dve.sem_inc(dve_went_on, 1)
                for k in range(KC):
                    done = e.bn_aggr(agg[:, k, :], stats[:, :, 4 * k:4 * k + 4, :].rearrange("p r t n -> p r (t n)"))
                done.then_inc(gn_step, 1)
                dve.wait_ge(gn_mean, 2 * img + 1)
                e.tensor_copy(mean_sb[:, :], ps_p[0][:, 0:KC]).then_inc(gn_step, 1)
                dve.wait_ge(gn_step, 6 * img + 2)
                e.tensor_tensor(gn[:, 0, :], agg[:, :, 0], mean_sb[:, :], ALU.subtract).then_inc(gn_step, 1)
                dve.wait_ge(gn_step, 6 * img + 3)
                e.tensor_tensor(gn[:, 1, :], gn[:, 0, :], gn[:, 0, :], ALU.mult).then_inc(gn_step, 1)
                dve.wait_ge(gn_step, 6 * img + 4)
                e.tensor_tensor(gn[:, 2, :], gn[:, 1, :], agg[:, :, 1], ALU.add).then_inc(gn_step, 1)
                dve.wait_ge(gn_mean, 2 * img + 2)
                e.tensor_scalar(gn[:, 3, :], ps_p[0][:, KC:2 * KC], GN_EPS, None, ALU.add).then_inc(gn_step, 1)

            def k_fill(F, j, i, rows=slice(WIN - BLK, WIN)):
                g, n = divmod(i, 2)
                dve.wait_ge(fill_hi, F + j + 1)
                for half in range(2):
                    r = slice(64 * half, 64 * half + 64)
                    at = (r, 2 * g + half, slice(HALO + 64 * n, HALO + 64 * n + 64), rows)
                    done = e.scalar_tensor_tensor(out=k_lo[at],
                                                  in0=ps_p[j % 4][r, 0:64 * (rows.stop - rows.start)]
                                                  .rearrange("p (c r) -> p c r", c=64),
                                                  scalar=SCALE / WS, in1=k_hi[at],
                                                  op0=ALU.mult, op1=ALU.subtract)
                done.then_inc(fill_lo, 1)

            def plain_fill(F, j, to, high, rows=P, cols=512):
                dve.wait_ge(fill_hi, F + j + 1)
                e.scalar_tensor_tensor(out=to, in0=ps_p[j % 4][0:rows, 0:cols], scalar=1.0 / WS, in1=high,
                                       op0=ALU.mult, op1=ALU.subtract).then_inc(fill_lo, 1)

            def place_bias(i, par):
                m = i // 2
                to, frm = ((qd_hi, b_hi), (qd_lo, b_lo))[i % 2]
                r, hq = slice(32 * m, 32 * m + 32), (m + 2) % 4
                return e.tensor_copy(to[r, hq // 2::2, par, :, hq % 2, :],
                                     frm[r, :, par, :].rearrange("p g (t q) -> p g t q", q=NQ))

            def produce(img, s, tail):
                F = fills_before(img, s)
                I = (img * ROWS + s - 1) * TURNS
                last = I - 1
                for j, (kind, i) in enumerate(ORDER):
                    if kind == "q":
                        plain_fill(F, j, q_lo[:, i % 2, i // 2, :], q_hi[:, i % 2, i // 2, :])
                        if tail and i == 0:
                            reciprocals(1)
                            normalise(last, 1)
                        if tail and i == 1:
                            context_lo(last)
                        if tail and i == 2:
                            add_output(last, TURNS - 1)
                        if tail:
                            if i == 0:
                                dve.wait_ge(fill_hi, F)
                                dve.wait_ge(fill_lo, F + 2)
                            r = slice(64 * (i // 2), 64 * (i // 2) + 64)
                            kk = (k_hi, k_lo)[i % 2]
                            done = e.tensor_copy(kk[r, i // 2::2, :, 0:WIN - BLK],
                                                 kk[r, i // 2::2, :, BLK:WIN])
                            if i == 3:
                                done.then_inc(k_down, 1)
                    elif kind == "b":
                        plain_fill(F, j, b_lo[:, i % 2, i // 2, :], b_hi[:, i % 2, i // 2, :])
                        if i >= 2:
                            for n in range(2):
                                done = place_bias(2 * i + n, 0)
                            if i == 3:
                                done.then_inc(bd_ready, 1)
                    elif kind == "k":
                        if tail and i == 0:
                            dve.wait_ge(k_down, img * (ROWS - 1) + s - 1)
                        k_fill(F, j, i)
                    elif i < 8:
                        plain_fill(F, j, v_lo[:, 2 * i:2 * i + 2, :].rearrange("p a c -> p (a c)"),
                                   v_hi[:, 2 * i:2 * i + 2, :].rearrange("p a c -> p (a c)"), CHUNK)
                        if i == 0 or i == 2:
                            dve.wait_ge(fill_lo, F + ORDER.index(("b", 1 if i == 0 else 3)) + 1 + 2)
                        for n in range(2):
                            if i < 2:
                                place_bias(2 * i + n, 0)
                            elif i < 6:
                                done = place_bias(2 * (i - 2) + n, 1)
                        if i == 5:
                            done.then_inc(bd_ready, 1)
                        if i == 5:
                            maxima(4 * I, 0)
                        if i == 6:
                            maxima(4 * I + 1, 1)
                    else:
                        plain_fill(F, j, v_lo[:, CHUNKS - 1, :], v_hi[:, CHUNKS - 1, :], CHUNK, C)

            def maxima(U, k):
                dve.wait_ge(scores_ready, U + 1)
                e.tensor_reduce(negmax[:, k, :], ps_s[k % 2][:, 0:2 * NKEY].rearrange("p (j n) -> p j n", j=2),
                                AX.X, ALU.max, negate=True).then_inc(max_ready, 1)

            def probs_lo(U, k):
                dve.wait_ge(pt_hi_done, U + 1)
                e.tensor_tensor(pt_lo[:, k % 2, :], ps_t[k % 2][0:CHUNK, :], pt_hi[:, k % 2, :],
                                ALU.subtract).then_inc(pt_lo_done, 1)

            def reciprocals(buf):
                e.reciprocal(rinv[:, :, :], rowsum[:, buf, :, :]).then_inc(rinv_done, 1)

            def normalise(I, buf):
                dve.wait_ge(rinv_done, I + 1)
                dve.wait_ge(context_done, 4 * I + 4 + 2)
                for half in range(2):
                    r = slice(64 * half, 64 * half + 64)
                    done = e.tensor_tensor(ctxn[r, :, :, :].rearrange("p a b d -> p (a b) d"),
                                           ps_c[buf][r, :].rearrange("p (u d) -> p u d", d=2 * DH)
                                           [:, :, DH * half:DH * half + DH],
                                           rinv[r, :, :].rearrange("p k j -> p (k j)").unsqueeze(2)
                                           .broadcast_to([64, 2 * PAIRS, DH]), ALU.mult)
                done.then_inc(norm_done, 1)

            def context_lo(I):
                dve.wait_ge(ct_hi_done, I + 1)
                e.tensor_tensor(ct_lo[:, :, :, :], ps_f[:, 0:256].rearrange("p (a h q) -> p a h q", a=2, h=2),
                                ct_hi[:, :, :, :], ALU.subtract).then_inc(ct_lo_done, 1)

            def add_output(I, t):
                dve.wait_ge(fc_done, I + 2)
                at = res[:, :, :, bass.ds(t * 2 * BLK, 2 * BLK)].rearrange("p k x c -> p (k x) c")
                e.scalar_tensor_tensor(out=at, in0=ps_f[:, 256:512].rearrange("p (m c) -> p m c", c=2 * BLK),
                                       scalar=1.0 / WS, in1=at, op0=ALU.mult, op1=ALU.add)\
                    .then_inc(out_added, 1)

            def turn(I, t, buf, r, first, last):
                for k in range(4):
                    U = 4 * I + k
                    if k == 2:
                        stats_piece(r, t, st_load)
                    if k == 0 and not first:
                        reciprocals(1 - buf)
                    if k < 2 or not last:
                        maxima(U + 2, (k + 2) % 4)
                    if k == 0 and not first:
                        normalise(I - 1, 1 - buf)
                    if k == 2 and not first:
                        context_lo(I - 1)
                    probs_lo(U, k)
                    if k == 3 and not first:
                        add_output(I - 1, t - 1)

            with dve.Fori(0, B) as img:
                group_stats(img)
                top_strip(img)
                for i in range(FILLS_K):
                    k_fill(img * IMG_FILLS, i, i, slice(0, WIN - BLK))

                def row(s, tail):
                    produce(img, s, tail)
                    rr = img * ROWS + s - 1
                    I = rr * TURNS
                    dve.wait_ge(res_ready, rr + 1)
                    dve.wait_ge(st_in, (ROWS // 2 + rr + 1) * 16)
                    turn(I, 0, 0, s - 1, True, False)
                    with dve.Fori(0, TURNS // 2 - 1) as t:
                        turn(I + 2 * t + 1, 2 * t + 1, 1, s - 1, False, False)
                        turn(I + 2 * t + 2, 2 * t + 2, 0, s - 1, False, False)
                    turn(I + TURNS - 1, TURNS - 1, 1, s - 1, False, True)

                row(1, False)
                with dve.Fori(2, ROWS + 1) as s:
                    row(s, True)
                I = (img + 1) * ROWS * TURNS - 1
                reciprocals(1)
                normalise(I, 1)
                context_lo(I)
                add_output(I, TURNS - 1)

        @block.tensor
        def _(pe):
            mm = nc.tensor.matmul
            pe.wait_ge(consts_in, 48)
            pe.wait_ge(zeroed, NZERO)
            pe.wait_ge(split_lo, 5)
            pe.wait_ge(onehot_in, 16 * PAIRS)

            def group_stats(img):
                pe.wait_ge(fill_lo, img * IMG_FILLS + 2)
                pe.wait_ge(gn_step, 6 * img + 1)
                mm(ps_p[0][:, 0:KC], gmean[:, :], agg[:, :, 0], start=True, stop=True).then_inc(gn_mean, 1)
                pe.wait_ge(gn_step, 6 * img + 5)
                mm(ps_p[0][:, KC:2 * KC], gmean[:, :], gn[:, 2, :], start=True, stop=True).then_inc(gn_mean, 1)

            def three(out_ap, terms, first=True, last=True):
                n = 3 * len(terms)
                i = 0
                for wh, wl, xh, xl in terms:
                    for a, b in ((wh, xh), (wh, xl), (wl, xh)):
                        done = mm(out_ap, a, b, start=first and i == 0, stop=last and i == n - 1,
                                  skip_group_check=True)
                        i += 1
                return done

            def bank_free(F, j):
                pe.wait_ge(fill_lo, F + (j - 4 + 1 if j >= 4 else 0) + 2)

            def k_fill(F, j, i, rows=slice(WIN - BLK, WIN)):
                g, n = divmod(i, 2)
                bank_free(F, j)
                cols = slice(HALO + 64 * n, HALO + 64 * n + 64)
                three(ps_p[j % 4][:, 0:64 * (rows.stop - rows.start)],
                      [(w_hi["k"][:, k, g * P:(g + 1) * P], w_lo["k"][:, k, g * P:(g + 1) * P],
                        xn_hi[:, k, cols, rows], xn_lo[:, k, cols, rows])
                       for k in range(KC)]).then_inc(fill_done, 1)

            def q_fill(F, j, i, I):
                par, g = divmod(i, 2)
                bank_free(F, j)
                if i == 3:
                    pe.wait_ge(norm_done, I + 2)

                def tokens(xn, k):
                    inside = xn[:, k, HALO:HALO + W, HALO:HALO + BLK]
                    return inside.rearrange("p (t a c) r -> p t a c r", a=2, c=BLK)[:, :, par, :, :]

                three(ps_p[j % 4][:, :],
                      [(w_hi["q"][:, k, g * P:(g + 1) * P], w_lo["q"][:, k, g * P:(g + 1) * P],
                        tokens(xn_hi, k), tokens(xn_lo, k)) for k in range(KC)]).then_inc(fill_done, 1)

            def v_fill(F, j, chunks):
                bank_free(F, j)
                for at, c in enumerate(chunks):
                    for n, (k, a, b) in enumerate([(k, a, b) for k in range(KC)
                                                   for a, b in ((0, 0), (0, 1), (1, 0))]):
                        src = ((xn_hi, xn_lo)[a])[:, k, :, :].rearrange("p c r -> p (c r)")
                        done = mm(ps_p[j % 4][0:CHUNK, at * C:(at + 1) * C],
                                  src[:, c * CHUNK:(c + 1) * CHUNK],
                                  (w_hi, w_lo)[b]["v"][:, k, :], start=n == 0, stop=n == 5,
                                  skip_group_check=True)
                done.then_inc(fill_done, 1)

            def b_fill(F, j, i):
                par, g = divmod(i, 2)
                bank_free(F, j)
                pe.wait_ge(fill_lo, F + i + 1 + 2)
                acc = ps_p[j % 4][:, :].rearrange("p (t y x) -> p t y x", y=BLK, x=BLK)
                qh = q_hi[:, g, par, :].rearrange("p (t y x) -> p t y x", y=BLK, x=BLK)
                ql = q_lo[:, g, par, :].rearrange("p (t y x) -> p t y x", y=BLK, x=BLK)
                for y in range(BLK):
                    n = par * BLK + y
                    three(acc[:, :, y, :], [(rel_hi[:, n, :], rel_lo[:, n, :], qh[:, :, y, :], ql[:, :, y, :])],
                          first=y == 0, last=False)
                for xx in range(BLK):
                    n = 2 * BLK + xx
                    done = three(acc[:, :, :, xx], [(rel_hi[:, n, :], rel_lo[:, n, :],
                                                     qh[:, :, :, xx], ql[:, :, :, xx])],
                                 first=False, last=xx == BLK - 1)
                done.then_inc(fill_done, 1)

            def produce(img, s, tail):
                F = fills_before(img, s)
                I = (img * ROWS + s - 1) * TURNS
                pe.wait_ge(xn_ready, img * ROWS + s)
                for j, (kind, i) in enumerate(ORDER):
                    if kind == "q":
                        q_fill(F, j, i, I)
                    elif kind == "b":
                        b_fill(F, j, i)
                    elif kind == "k":
                        k_fill(F, j, i)
                    elif i < 8:
                        v_fill(F, j, (2 * i, 2 * i + 1))
                    else:
                        v_fill(F, j, (CHUNKS - 1,))
                    if (kind, i) == ("v", 5):
                        pe.wait_ge(qd_hi_ready, 2 * (img * ROWS + s) - 1)
                        pe.wait_ge(qd_lo_ready, 2 * (img * ROWS + s) - 1)
                        pe.wait_ge(bd_ready, 2 * (img * ROWS + s) - 1)
                        pe.wait_ge(fill_lo, F + ORDER.index(("k", 3)) + 1 + 2)
                        pe.wait_ge(exp_done, 4 * I + 2)
                        scores(4 * I, 0, 0)
                        scores(4 * I + 1, 1, 0)
                    if tail and (kind, i) == ("q", 0):
                        context(4 * I - 2, 2, TURNS - 1, I - 1)
                        context(4 * I - 1, 3, TURNS - 1, I - 1)
                    if tail and (kind, i) == ("q", 1):
                        transpose_context(I - 1)
                    if tail and (kind, i) == ("q", 2):
                        output(I - 1)
                pe.wait_ge(fill_lo, F + FILLS - 1 + 2)

            def scores(U, k, t):
                par, g = divmod(k, 2)
                for j in range(2):
                    p = 2 * g + j

                    def queries(qd):
                        return qd[:, p, par, :, :, :].rearrange("p t h q -> p (t h q)")[
                            :, bass.ds(t * 2 * NQ, 2 * NQ)]

                    def keys(kk):
                        return kk[:, p, :, :].rearrange("p c r -> p (c r)")[
                            :, bass.ds((2 * t + par) * CHUNK, NKEY)]

                    done = three(ps_s[k % 2][:, j * NKEY:(j + 1) * NKEY],
                                 [(queries(qd_hi), queries(qd_lo), keys(k_hi), keys(k_lo))])
                done.then_inc(scores_ready, 1)

            def transpose_probs(U, k):
                for j in range(2):
                    for c in range(2):
                        at = (2 * j + c) * P
                        done = nc.tensor.transpose(ps_t[k % 2][0:CHUNK, at:at + P],
                                                   prob[:, k % 2, j, c * CHUNK:(c + 1) * CHUNK], ident[:, :])
                done.then_inc(probT_ready, 1)

            def context(U, k, t, I):
                par, g = divmod(k, 2)
                pe.wait_ge(pt_lo_done, U + 3)
                for j in range(2):
                    p = 2 * g + j
                    terms = []
                    for c in range(2):
                        at = (2 * j + c) * P

                        def values(v):
                            return v[:, bass.ds(2 * t + par + c, 1), p * 2 * DH:(p + 1) * 2 * DH]\
                                .rearrange("p a c -> p (a c)")

                        terms.append((pt_hi[:, k % 2, at:at + P], pt_lo[:, k % 2, at:at + P],
                                      values(v_hi), values(v_lo)))
                    at = (par * PAIRS + p) * 2 * DH
                    done = three(ps_c[t % 2][:, at:at + 2 * DH], terms)
                done.then_inc(context_done, 1)

            def transpose_context(I):
                pe.wait_ge(norm_done, I + 3)
                pe.wait_ge(out_added, I + 1)
                for par in range(2):
                    done = nc.tensor.transpose(ps_f[:, par * P:(par + 1) * P],
                                               ctxn[:, par, :, :].rearrange("p a d -> p (a d)"), ident[:, :])
                done.then_inc(ctxT_ready, 1)

            def output(I):
                pe.wait_ge(ct_lo_done, I + 1)

                def tokens(ct, half):
                    return ct[:, :, half, :].rearrange("p a (y x) -> p x a y", y=BLK)

                for k in range(KC):
                    done = three(ps_f[:, 256 + k * P:256 + (k + 1) * P],
                                 [(w_hi["o"][:, half, k * P:(k + 1) * P], w_lo["o"][:, half, k * P:(k + 1) * P],
                                   tokens(ct_hi, half), tokens(ct_lo, half)) for half in range(2)])
                done.then_inc(fc_done, 1)

            def turn(I, t, first, last):
                for k in range(4):
                    U = 4 * I + k
                    pe.wait_ge(exp_done, U + 1 + 2)
                    if k < 2:
                        scores(U + 2, k + 2, t)
                    elif not last:
                        scores(U + 2, k - 2, t + 1)
                    transpose_probs(U, k)
                    if k == 1 and not first:
                        transpose_context(I - 1)
                    if k == 3 and not first:
                        output(I - 1)
                    if k > 0:
                        if k < 3 or not last:
                            context(U - 1, k - 1, t, I)
                    elif not first:
                        context(U - 1, 3, t - 1, I - 1)

            with pe.Fori(0, B) as img:
                group_stats(img)
                pe.wait_ge(xn_ready, img * ROWS + 1)
                for i in range(FILLS_K):
                    k_fill(img * IMG_FILLS, i, i, slice(0, WIN - BLK))

                def row(s, tail):
                    produce(img, s, tail)
                    rr = img * ROWS + s - 1
                    I = rr * TURNS
                    pe.wait_ge(qd_hi_ready, 2 * rr + 2)
                    pe.wait_ge(qd_lo_ready, 2 * rr + 2)
                    pe.wait_ge(bd_ready, 2 * rr + 2)
                    for t in range(TURNS):
                        turn(I + t, t, t == 0, t == TURNS - 1)

                row(1, False)
                with pe.Fori(2, ROWS + 1) as s:
                    row(s, True)
                I = (img + 1) * ROWS * TURNS
                context(4 * I - 2, 2, TURNS - 1, I - 1)
                context(4 * I - 1, 3, TURNS - 1, I - 1)
                transpose_context(I - 1)
                output(I - 1)


def _relative_weights(np, rel_w, rel_h):
    full = np.zeros((P, NREL, P), np.float32)
    for m in range(4):
        hq = (m + 2) % 4
        rows = slice(DH * hq, DH * hq + DH)
        for n in range(NREL):
            q = n % BLK
            for j in range(WIN):
                if n < 2 * BLK:
                    full[rows, n, 32 * m + (j + BLK * (n // BLK)) % 16] = rel_w[j - q + WIN - 1]
                else:
                    full[rows, n, 32 * m + 16 + j] = rel_h[j - q + WIN - 1]
    return full.reshape(P, NREL * P)


def kernel(**inputs):
    import numpy as _np
    import concourse.bacc as _bacc
    from concourse import mybir as _mybir
    from concourse.bass_utils import run_bass_kernel_spmd as _run

    a = {n: _np.asarray(v) for n, v in inputs.items()}
    x, w_q, w_kv = a["x"], a["L0_conv_w_q"], a["L0_conv_w_kv"]
    fc_w, fc_b = a["L0_conv_fc_w"], a["L0_conv_fc_b"]

    def halves(w):
        return w.T.reshape(KC, P, C).transpose(1, 0, 2).reshape(P, KC * C)

    fc = fc_w.T.reshape(PAIRS, 2, DH, C).transpose(1, 0, 2, 3).reshape(KC, P, C)
    col, row = _np.arange(WP)[:, None], _np.arange(WIN)[None, :]
    onehot = _np.zeros((P, WP, WIN), _np.float16)
    for m in range(4):
        for r in range(16):
            onehot[32 * m + r] = (col % 16 == r) & (row >= 0)
        for i in range(WIN):
            onehot[32 * m + 16 + i] = (row == i) & (col >= 0)
    gmean = _np.kron(_np.eye(P // CG), _np.full((CG, CG), 1.0 / CG)).astype(_np.float32)
    arrays = {
        "x": x, "wqT": halves(w_q), "wkT": halves(w_kv[:C]), "wvT": halves(w_kv[C:]),
        "fcT": fc.transpose(1, 0, 2).reshape(P, KC * C), "fcb": fc_b.reshape(KC, P).T,
        "rel": _relative_weights(_np, a["L0_conv_rel_w"], a["L0_conv_rel_h"]), "onehot": onehot,
        "ident": _np.eye(P, dtype=_np.float32), "gmean": gmean,
    }
    arrays = {n: _np.ascontiguousarray(v) for n, v in arrays.items()}
    nc = _bacc.Bacc("TRN2", target_bir_lowering=False, num_devices=1)
    args = [nc.dram_tensor(f"in_{n}", v.shape, _mybir.dt.from_np(v.dtype), kind="ExternalInput").ap()
            for n, v in arrays.items()]
    args.append(nc.dram_tensor("out_0", x.shape, _mybir.dt.float32, kind="ExternalOutput").ap())
    halo_attention_program(nc, *args)
    r = _run(nc, [{f"in_{n}": v for n, v in arrays.items()}], core_ids=[0])
    return r.results[0]["out_0"]
```
